# Optimizing a Trainium2 kernel written in Bass

```python
import numpy as np
import jax
import jax.numpy as jnp

def _softmax(x, axis=-1):
    return jax.nn.softmax(x, axis=axis)

def _gelu(x):
    return jax.nn.gelu(x, approximate=True)

def _silu(x):
    return jax.nn.silu(x)

def _sigmoid(x):
    return jax.nn.sigmoid(x)

def _layernorm(x, axis=-1, eps=1e-05):
    m = jnp.mean(x, axis=axis, keepdims=True)
    v = jnp.var(x, axis=axis, keepdims=True)
    return (x - m) / jnp.sqrt(v + eps)

def _scatter_add(tgt, idx, src, axis=0):
    return tgt.at[idx].add(src)

def _segment_sum(src, seg, n):
    return jax.ops.segment_sum(src, seg, n)
kernel_name = 'mk_gnn_resnorm_d2_gnn_r64_5e4c06'

def setup_inputs(seed: int=0):
    np.random.seed(seed)
    _w = jnp.asarray

    def _rec_inputs():
        import jax
        import jax.numpy as jnp
        _gk = jax.random.key(seed)
        x = -0.0002117 + 1 * jax.random.normal(jax.random.fold_in(_gk, 1), (50000, 128), jnp.float32)
        src = jax.random.randint(jax.random.fold_in(_gk, 2), (12500,), 0, 50000, jnp.int32)
        dst = jnp.minimum((50000 * jax.random.uniform(jax.random.fold_in(_gk, 3), (12500,)) ** 2.0).astype(jnp.int32), 49999)
        _o = jnp.argsort(dst, stable=True)
        src = src[_o]
        dst = dst[_o]
        edge_attr_128 = 5.93493e-05 + 1.00006 * jax.random.normal(jax.random.fold_in(_gk, 11), (12500, 128), jnp.float32)
        return (x, src, dst, edge_attr_128)
    x, src, dst, edge_attr_128 = _rec_inputs()

    def _L0_gnn_setup():
        import jax, jax.numpy as jnp
        import numpy as np
        N_NODES = 3125
        N_EDGES = 9375
        D = 128
        L = 3
        BN_EPS = 1e-05
        key = jax.random.key(seed)
        ks = jax.random.split(key, 8)
        x = jax.random.normal(ks[0], (N_NODES, D), dtype=jnp.float32)
        edge_index = jax.random.randint(ks[1], (2, N_EDGES), 0, N_NODES)
        edge_attr = jax.random.normal(ks[2], (N_EDGES, D), dtype=jnp.float32)
        W1 = jax.random.normal(ks[3], (L, D, 2 * D), dtype=jnp.float32) * (1.0 / np.sqrt(D))
        b1 = jnp.zeros((L, 2 * D), dtype=jnp.float32)
        gamma = jnp.ones((L, 2 * D), dtype=jnp.float32)
        beta = jnp.zeros((L, 2 * D), dtype=jnp.float32)
        W2 = jax.random.normal(ks[4], (L, 2 * D, D), dtype=jnp.float32) * (1.0 / np.sqrt(2 * D))
        b2 = jnp.zeros((L, D), dtype=jnp.float32)
        eps = jnp.zeros((L,), dtype=jnp.float32)
        lin_w = jax.random.normal(ks[5], ((L + 1) * D, D), dtype=jnp.float32) * (1.0 / np.sqrt((L + 1) * D))
        lin_b = jnp.zeros((D,), dtype=jnp.float32)
        return {'x': x, 'edge_index': edge_index, 'edge_attr': edge_attr, 'eps': eps, 'W1': W1, 'b1': b1, 'gamma': gamma, 'beta': beta, 'W2': W2, 'b2': b2, 'lin_w': lin_w, 'lin_b': lin_b}
    _L0_gnn_all = _L0_gnn_setup()
    _L0_gnn_in = {k: v for k, v in _L0_gnn_all.items() if k in ('eps', 'W1', 'b1', 'gamma', 'beta', 'W2', 'b2', 'lin_w', 'lin_b')}
    del _L0_gnn_all

    def _L1_gnn_setup():
        import jax, jax.numpy as jnp
        import numpy as np
        key = jax.random.key(seed)
        k1, k2, k3 = jax.random.split(key, 3)
        N, E, D_IN, D_OUT = (50000, 12500, 128, 128)
        x = jax.random.normal(k1, (N, D_IN), dtype=jnp.float32)
        edge_index = jax.random.randint(k2, (2, E), 0, N, dtype=jnp.int64)
        W = jax.random.normal(k3, (D_OUT, D_IN), dtype=jnp.float32) * (1.0 / np.sqrt(D_IN))
        return {'x': x, 'edge_index': edge_index, 'W': W}
    _L1_gnn_all = _L1_gnn_setup()
    _L1_gnn_in = {k: v for k, v in _L1_gnn_all.items() if k in ('W',)}
    del _L1_gnn_all
    return {'x': x, 'src': src, 'dst': dst, 'edge_attr_128': edge_attr_128, 'L0_gnn_eps': _L0_gnn_in['eps'], 'L0_gnn_W1': _L0_gnn_in['W1'], 'L0_gnn_b1': _L0_gnn_in['b1'], 'L0_gnn_gamma': _L0_gnn_in['gamma'], 'L0_gnn_beta': _L0_gnn_in['beta'], 'L0_gnn_W2': _L0_gnn_in['W2'], 'L0_gnn_b2': _L0_gnn_in['b2'], 'L0_gnn_lin_w': _L0_gnn_in['lin_w'], 'L0_gnn_lin_b': _L0_gnn_in['lin_b'], 'L1_gnn_W': _L1_gnn_in['W']}

def reference(x, src, dst, edge_attr_128, L0_gnn_eps, L0_gnn_W1, L0_gnn_b1, L0_gnn_gamma, L0_gnn_beta, L0_gnn_W2, L0_gnn_b2, L0_gnn_lin_w, L0_gnn_lin_b, L1_gnn_W):
    import jax
    import jax.numpy as jnp

    def _L0_gnn_ref(x, edge_index, edge_attr, eps, W1, b1, gamma, beta, W2, b2, lin_w, lin_b):
        import jax, jax.numpy as jnp
        import numpy as np
        N_NODES = 3125
        N_EDGES = 9375
        D = 128
        L = 3
        BN_EPS = 1e-05
        n = x.shape[0]
        src, dst = (edge_index[0], edge_index[1])
        h = x
        h_list = [x]
        for l in range(W1.shape[0]):
            msg = jax.nn.relu(h[src] + edge_attr)
            agg = jax.ops.segment_sum(msg, dst, num_segments=n)
            z = (1.0 + eps[l]) * h + agg
            u = z @ W1[l] + b1[l]
            mu = u.mean(axis=0)
            var = u.var(axis=0)
            u = gamma[l] * (u - mu) * jax.lax.rsqrt(var + BN_EPS) + beta[l]
            u = jax.nn.relu(u)
            h = jax.nn.relu(u @ W2[l] + b2[l])
            h_list.append(h)
        rep = jnp.concatenate(h_list, axis=1)
        return rep @ lin_w + lin_b

    def _L1_gnn_ref(x, edge_index, W):
        import jax, jax.numpy as jnp
        import numpy as np
        h = x @ W.T
        N = x.shape[0]
        src, dst = (edge_index[0], edge_index[1])
        agg = jax.ops.segment_sum(h[src], dst, num_segments=N)
        return agg + h
    edge_index = jnp.stack([src, dst])
    x = _layernorm(x + _L0_gnn_ref(x, edge_index, edge_attr_128, L0_gnn_eps, L0_gnn_W1, L0_gnn_b1, L0_gnn_gamma, L0_gnn_beta, L0_gnn_W2, L0_gnn_b2, L0_gnn_lin_w, L0_gnn_lin_b), axis=-1)
    x = _layernorm(x + _L1_gnn_ref(x, edge_index, L1_gnn_W), axis=-1)
    return x

_drawn_inputs = setup_inputs


def setup_inputs(seed=0):
    import zlib

    import numpy as np

    out = dict(_drawn_inputs(seed))
    spreads = {'L0_gnn_eps': (0.0, 0.8),
     'L0_gnn_b1': (0.0, 0.8),
     'L0_gnn_gamma': (1.0, 0.2),
     'L0_gnn_beta': (0.0, 0.1),
     'L0_gnn_b2': (0.0, 0.1),
     'L0_gnn_lin_b': (0.0, 0.1)}
    factors = {}
    for name, (base, spread) in spreads.items():
        noise = np.random.default_rng([zlib.crc32(name.encode()), seed]).standard_normal(out[name].shape)
        drawn = base * np.exp(spread * noise) if base else spread * noise
        out[name] = jnp.asarray(drawn.astype(out[name].dtype))
    for name, factor in factors.items():
        out[name] = (out[name] * factor).astype(out[name].dtype)
    return out
```

```python
from contextlib import ExitStack

import concourse.bass as bass
from concourse import mybir

F32 = mybir.dt.float32
I32 = mybir.dt.int32
BF16 = mybir.dt.bfloat16
ALU = mybir.AluOpType
ACT = mybir.ActivationFunctionType

P = 128
D = 128
NODES = 50000
EDGES = 12500
LAYERS = 3
R = 4
GROUP = P * R
GROUPS = -(-NODES // GROUP)
PAIRS = GROUPS // 2
ROWS = GROUPS * GROUP
TAIL_P = (NODES - (GROUPS - 1) * GROUP) // R
TILES = -(-EDGES // P)
TAIL_E = EDGES - (TILES - 1) * P
CT = 7
CPAIRS = TILES // CT // 2
FAR = 1 << 20
INV_N = 1.0 / NODES
EPS = 1e-5
ZCOLS = 2000
ZPARTS = ROWS * D // P // ZCOLS
ZREST = ROWS * D // P - ZPARTS * ZCOLS
HALVES = ((0, 4), (4, 7))
BATCH_DMAS = 7
BN_STEPS = 16


def steps(eng, end):
    yield 0
    with eng.Fori(1, end) as i:
        yield i


def gnn_kernel(nc, x, src, dst, edge_attr, eps, W1, b1, gamma, beta, W2, b2, lin_w, lin_b, Wc, out):
    ds = bass.ds
    H = [None] + [nc.dram_tensor(f"h{l}_rows", [GROUPS, P, R * D], F32).ap() for l in range(1, LAYERS + 1)]
    AGG = nc.dram_tensor("agg_rows", [GROUPS, P, R * D], F32).ap()
    GR = nc.dram_tensor("g_rows", [GROUPS, P, R * D], F32).ap()
    SR = nc.dram_tensor("s_rows", [GROUPS, P, R * D], F32).ap()
    LAST = nc.dram_tensor("last_rows_dram", [1, TILES, D], F32).ap()
    H_flat = [x] + [h.rearrange("g p (r d) -> (g p r) d", r=R) for h in H[1:]]
    AGG_flat = AGG.rearrange("g p (r d) -> (g p r) d", r=R)
    GR_flat = GR.rearrange("g p (r d) -> (g p r) d", r=R)
    SR_flat = SR.rearrange("g p (r d) -> (g p r) d", r=R)
    BODY = (GROUPS - 1) * GROUP
    x_groups = x[0:BODY, :].rearrange("(g p r) d -> g p r d", p=P, r=R)
    x_tail = x[BODY:NODES, :].rearrange("(p r) d -> p r d", r=R)
    out_groups = out[0:BODY, :].rearrange("(g p r) d -> g p (r d)", p=P, r=R)
    out_tail = out[BODY:NODES, :].rearrange("(p r) d -> p (r d)", r=R)
    ea_tiles = edge_attr[0:(TILES - 1) * P, :].rearrange("(t p) d -> p t d", p=P)

    with ExitStack() as ctx:
        def sb(name, shape, dt=F32):
            return ctx.enter_context(nc.sbuf_tensor(name, shape, dt))

        def sem(name):
            return ctx.enter_context(nc.semaphore(name))

        def sems(name, n=2):
            return [sem(f"{name}{k}") for k in range(n)]

        def bufs(name, shape, dt=F32):
            return [sb(f"{name}{k}", shape, dt) for k in range(2)]

        ident = sb("ident", [P, P])
        eq_all = sb("eq_all", [P, TILES * P], BF16)
        sel_all = sb("sel_all", [TILES, TILES * P], BF16)
        zeros = sb("zeros", [P, ZCOLS])
        id_rows = sb("id_rows", [TILES, 3, P], I32)
        id_float = sb("id_float", [TILES, 4, P])
        same_next = sb("same_next", [TILES, P])
        dst_c = sb("dst_c", [P, TILES])
        rep_c = sb("rep_c", [P, TILES])
        src_i = sb("src_i", [P, TILES], I32)
        dst_i = sb("dst_i", [P, TILES], I32)
        put_i = sb("put_i", [P, TILES], I32)
        w1 = sb("w1", [P, 2 * D])
        w2 = sb("w2", [P, 2, D])
        lin = sb("lin", [P, LAYERS + 1, D])
        wc_in = sb("wc_in", [P, D])
        wcT = sb("wcT", [P, D])
        b2_bc = sb("b2_bc", [P, 1, D])
        linb_bc = sb("linb_bc", [P, 1, D])
        bn_in = sb("bn_in", [P, 3, 2])
        eps_in = sb("eps_in", [P, 1])
        self_w = sb("self_w", [P, 2])
        gram = sb("gram", [P, D + 1])
        cross = sb("cross", [P, D + 1])
        zz = sb("zz", [P, D])
        zmean = sb("zmean", [P, 1])
        zw = sb("zw", [P, 2 * D])
        ones = sb("ones", [P, 1])
        eps_c = sb("eps_c", [P, 1])
        bn_mu = sb("bn_mu", [P, 2])
        bn_sq = sb("bn_sq", [P, 2])
        bn_var = sb("bn_var", [P, 2])
        bn_std = sb("bn_std", [P, 2])
        bn_scale = sb("bn_scale", [P, 2])
        bn_bias = sb("bn_bias", [P, 2])
        A = sb("A", [P, TILES, D])
        last_rows = sb("last_rows", [TILES, D])
        got = bufs("got", [P, CT, D])
        ea = bufs("ea", [P, CT, D])
        msg = bufs("msg", [P, CT, D])
        sel = bufs("sel", [P, CT * P])
        tot = bufs("tot", [P, CT, D])
        mix = bufs("mix", [P, CT, D + 2])
        get_ix = bufs("get_ix", [P, CT], I32)
        put_ix = bufs("put_ix", [P, CT], I32)
        estat = sb("estat", [P, CT, 6])
        emv = sb("emv", [P, CT, 2])
        estd = sb("estd", [P, CT])
        enm = sb("enm", [P, CT])
        hrow = bufs("hrow", [P, R * D])
        arow = bufs("arow", [P, R * D])
        z = bufs("z", [P, R * D])
        zT = bufs("zT", [P, R * D])
        vT = bufs("vT", [P, 2, R * D])
        hsum = bufs("hsum", [P, R, D])
        hp = bufs("hp", [P, R, D + 4])
        fh = [[A[:, (4 * (4 * k + y)):(4 * (4 * k + y)) + 4, :] for y in range(4)] for k in range(2)]
        fT = [A[:, 32 + 16 * k:48 + 16 * k, :] for k in range(2)]
        fstat = [sb(f"fstat{k}", [P, 2, R, 6]) for k in range(2)]
        fmv = [sb(f"fmv{k}", [P, 2, R, 2]) for k in range(2)]
        fstd = [sb(f"fstd{k}", [P, 2, R]) for k in range(2)]
        fnm = [sb(f"fnm{k}", [P, 2, R]) for k in range(2)]
        fy = hsum
        fx2 = [t[:, 0:R, :] for t in msg]
        fx2T = z
        fg = hrow
        fs = [t[:, 0:R, :] for t in got]
        fo = [t[:, 0:R, :] for t in ea]

        psZ = ctx.enter_context(nc.psum_tensor("psZ", [P, 512], F32))
        psU = ctx.enter_context(nc.psum_tensor("psU", [P, 4, 512], F32))
        psH = [ctx.enter_context(nc.psum_tensor(f"psH{k}", [P, 512], F32)) for k in range(2)]
        psG = ctx.enter_context(nc.psum_tensor("psG", [P, 512], F32))

        ids_in = sem("ids_in"); ids_pad = sem("ids_pad"); consts = sem("consts"); passed = sem("passed"); ident_up = sem("ident_up")
        const_in = sem("const_in"); bc_in = sem("bc_in"); zeroed = sem("zeroed"); zero_tile = sem("zero_tile")
        ids_done = sem("ids_done"); ids_T = sem("ids_T"); sel_raw = sem("sel_raw"); sel_done = sem("sel_done")
        tables = sem("tables"); wcT_up = sem("wcT_up"); dve_step = sem("dve_step"); bc_pad = sem("bc_pad")
        x_in = sems("x_in")
        weights_in = sem("weights_in"); staged = sem("staged")
        src_in = sems("src_in"); ea_in = sems("ea_in"); ea_tail_in = sem("ea_tail_in")
        msg_up = sems("msg_up"); sel_up = sems("sel_up"); tile_sum = sems("tile_sum"); a_up = sems("a_up")
        last_in = sem("last_in"); last_out = sem("last_out"); carry_sum = sems("carry_sum"); dst_in = sems("dst_in")
        tot_up = sems("tot_up"); put_done = sems("put_done"); mix_up = sems("mix_up"); cross_sum = sems("cross_sum")
        cross_add = sem("cross_add"); got_used = sems("got_used"); got_scaled = sems("got_scaled")
        cross_T = sem("cross_T"); zz_up = sem("zz_up"); zzw = sem("zzw"); zw_up = sem("zw_up"); bn_sums = sem("bn_sums")
        bn_var_up = sem("bn_var_up"); bn_std_up = sem("bn_std_up"); bn_up = sem("bn_up")
        rows_in = sems("rows_in"); z_up = sems("z_up"); z_T = sems("z_T"); zT_up = sems("zT_up")
        u_up = sems("u_up"); v_up = sems("v_up"); h_sum = sems("h_sum"); h_bias = sems("h_bias"); h_up = sems("h_up")
        gram_up = sems("gram_up"); gram_add = sem("gram_add"); stored = sems("stored")
        f_in = sems("f_in"); f_T = sems("f_T"); f_copied = sems("f_copied"); f_lin = sems("f_lin"); f_y = sems("f_y")
        f_bias = sems("f_bias"); f_stat = sems("f_stat"); f_rec = sems("f_rec"); f_var = sems("f_var"); f_std = sems("f_std"); f_norm = sems("f_norm"); f_x2 = sems("f_x2")
        f_x2T = sems("f_x2T"); f_x2c = sems("f_x2c"); f_w = sems("f_w"); f_g = sems("f_g"); f_s = sems("f_s"); f_o = sems("f_o")
        f_stored = sems("f_stored"); e_y = sem("e_y"); e_stat = sem("e_stat"); e_var = sem("e_var"); e_std = sem("e_std"); e_rec = sem("e_rec"); e_nm = sem("e_nm"); bn_step = sem("bn_step"); out_done = sems("out_done")

        def plain(eng):
            eng.sem_inc(passed, 1)

        block = ctx.enter_context(nc.Block())

        @block.sync
        def _(sp):
            sp.wait_ge(ids_pad, 1)
            whole = (TILES - 1) * P
            for slot, ids in ((0, dst), (2, src)):
                sp.dma_start(id_rows[0:TILES - 1, slot, :], ids[0:whole].rearrange("(t p) -> t p", p=P)).then_inc(ids_in, 16)
                sp.dma_start(id_rows[TILES - 1:TILES, slot, 0:TAIL_E], ids[whole:EDGES].rearrange("(t p) -> t p", t=1)).then_inc(ids_in, 16)
            sp.dma_start(id_rows[0:TILES - 1, 1, :], dst[1:whole + 1].rearrange("(t p) -> t p", p=P)).then_inc(ids_in, 16)
            sp.dma_start(id_rows[TILES - 1:TILES, 1, 0:TAIL_E - 1], dst[whole + 1:EDGES].rearrange("(t p) -> t p", t=1)).then_inc(ids_in, 16)
            sp.wait_ge(bc_pad, 1)
            flat = A[:, :, :].rearrange("p t d -> p (t d)").bitcast(I32)
            sp.dma_start(flat[:, 0:EDGES], dst.partition_broadcast(P)).then_inc(bc_in, 16)
            sp.dma_start(lin[:, :, :], lin_w.rearrange("(y k) d -> k y d", k=D)).then_inc(const_in, 16)
            sp.dma_start(wc_in[:, :], Wc).then_inc(const_in, 16)
            sp.dma_start(linb_bc[:, 0, :], lin_b.partition_broadcast(P)).then_inc(const_in, 16)
            sp.wait_ge(zero_tile, 1)
            agg_parts = AGG.rearrange("g p n -> (g p n)").rearrange("(p n) -> p n", p=P)
            with sp.Fori(0, ZPARTS) as i:
                sp.dma_start(agg_parts[:, ds(i * ZCOLS, ZCOLS)], zeros[:, :]).then_inc(zeroed, 16)
            if ZREST:
                sp.dma_start(agg_parts[:, ZPARTS * ZCOLS:], zeros[:, 0:ZREST]).then_inc(zeroed, 16)

            sp.wait_ge(ident_up, 1)
            def load_x(i, k, tail=False):
                sp.wait_ge(gram_up[k], i)
                if tail:
                    sp.dma_start(hp[k][0:TAIL_P, :, 0:D], x_tail).then_inc(x_in[k], 16)
                else:
                    sp.dma_start(hp[k][:, :, 0:D], x_groups[ds(2 * i + k, 1), :, :, :].rearrange("o p r d -> (o p) r d")).then_inc(x_in[k], 16)

            for i in steps(sp, PAIRS - 1):
                for k in range(2):
                    load_x(i, k)
            load_x(PAIRS - 1, 0)
            load_x(PAIRS - 1, 1, tail=True)

            def load_ea(l, j, k, last=False):
                sp.wait_ge(msg_up[k], l * CPAIRS + j)
                c = (2 * j + k) * CT
                if last:
                    sp.dma_start(ea[k][:, 0:CT - 1, :], ea_tiles[:, c:c + CT - 1, :]).then_inc(ea_in[k], 16)
                    sp.dma_start(ea[k][0:TAIL_E, CT - 1, :], edge_attr[(TILES - 1) * P:EDGES, :]).then_inc(ea_tail_in, 16)
                else:
                    sp.dma_start(ea[k][:, :, :], ea_tiles[:, ds(c, CT), :]).then_inc(ea_in[k], 16)

            def load_last_rows(l):
                for k in range(2):
                    sp.wait_ge(a_up[k], 2 * CPAIRS * (l + 1))
                sp.dma_start(LAST, A[P - 1:P, :, :]).then_inc(last_out, 16)
                sp.wait_ge(last_out, 16 * (l + 1))
                sp.dma_start(last_rows[:, :], LAST.rearrange("o t d -> (o t) d")).then_inc(last_in, 16)

            def h_group(y, g, to, done, tail=False):
                if y:
                    sp.dma_start(to, H[y][ds(g, 1), :, :].rearrange("o p (r d) -> (o p) r d", r=R)).then_inc(done, 16)
                elif tail:
                    sp.dma_start(to[0:TAIL_P], x_tail).then_inc(done, 16)
                else:
                    sp.dma_start(to, x_groups[ds(g, 1), :, :, :].rearrange("o p r d -> (o p) r d")).then_inc(done, 16)

            def load_rows(l, n, i, last=False):
                for k in range(2):
                    sp.wait_ge(z_up[k], n)
                    g = 2 * i + k
                    h_group(l, g, hrow[k][:, :].rearrange("p (r d) -> p r d", d=D), rows_in[k], last and k == 1)
                    sp.dma_start(arow[k][:, :], AGG[ds(g, 1), :, :].rearrange("o p n -> (o p) n")).then_inc(rows_in[k], 16)

            def store_pair(l, i):
                n = l * PAIRS + i
                for k in range(2):
                    sp.wait_ge(h_up[k], n + 1)
                    sp.dma_start(H[l + 1][ds(2 * i + k, 1), :, :].rearrange("o p (r d) -> (o p) r d", r=R),
                                 hp[k][:, :, 0:D]).then_inc(stored[k], 16)

            for l in range(LAYERS):
                for k in range(2):
                    if l:
                        sp.wait_ge(stored[k], 16 * PAIRS * l)
                sp.dma_start(w1[:, :], W1[l]).then_inc(weights_in, 16)
                sp.dma_start(w2[:, :, :], W2[l].rearrange("(c k) n -> k c n", c=2)).then_inc(weights_in, 16)
                for row, vec in enumerate((b1, gamma, beta)):
                    with nc.allow_non_contiguous_dma("256 features"):
                        sp.dma_start(bn_in[:, row, :], vec[l].rearrange("(c f) -> f c", c=2)).then_inc(weights_in, 16)
                sp.dma_start(b2_bc[:, 0, :], b2[l].partition_broadcast(P)).then_inc(weights_in, 16)
                sp.dma_start(eps_in[:, :], eps[l:l + 1].partition_broadcast(P)).then_inc(weights_in, 16)
                for j in steps(sp, CPAIRS - 1):
                    for k in range(2):
                        load_ea(l, j, k)
                load_ea(l, CPAIRS - 1, 0)
                load_ea(l, CPAIRS - 1, 1, last=True)
                load_last_rows(l)
                for k in range(2):
                    sp.wait_ge(put_done[k], 16 * CT * CPAIRS * (l + 1))
                sp.wait_ge(zeroed, 16 * (ZPARTS + (ZREST > 0)))
                load_rows(l, l * PAIRS, 0)
                load_rows(l, l * PAIRS + 1, 1)
                for i in steps(sp, PAIRS - 3):
                    load_rows(l, l * PAIRS + i + 2, i + 2)
                    store_pair(l, i)
                load_rows(l, (l + 1) * PAIRS - 1, PAIRS - 1, last=True)
                store_pair(l, PAIRS - 3)
                store_pair(l, PAIRS - 2)
                store_pair(l, PAIRS - 1)

            for k in range(2):
                sp.wait_ge(stored[k], 16 * PAIRS * LAYERS)

            def load_f(i, k, last=False):
                sp.wait_ge(f_lin[k], i)
                sp.wait_ge(f_y[k], i)
                for y in range(LAYERS + 1):
                    h_group(y, 2 * i + k, fh[k][y], f_in[k], last and k == 1)

            def store_f(i, k, tail=False):
                sp.wait_ge(f_g[k], i + 1)
                sp.dma_start(GR[ds(2 * i + k, 1), :, :].rearrange("o p n -> (o p) n"), fg[k][:, :]).then_inc(f_stored[k], 16)
                sp.wait_ge(f_s[k], i + 1)
                sp.dma_start(SR[ds(2 * i + k, 1), :, :].rearrange("o p (r d) -> (o p) r d", r=R), fs[k]).then_inc(f_stored[k], 16)
                sp.wait_ge(f_o[k], i + 1)
                if tail:
                    sp.dma_start(out_tail.rearrange("p (r d) -> p r d", r=R), fo[k][0:TAIL_P]).then_inc(f_stored[k], 16)
                else:
                    sp.dma_start(out_groups[ds(2 * i + k, 1), :, :].rearrange("o p (r d) -> (o p) r d", r=R), fo[k]).then_inc(f_stored[k], 16)

            load_f(0, 0)
            load_f(0, 1)
            for i in steps(sp, PAIRS - 2):
                for k in range(2):
                    load_f(i + 1, k)
                    store_f(i, k)
            for k in range(2):
                load_f(PAIRS - 1, k, last=True)
                store_f(PAIRS - 2, k)
            store_f(PAIRS - 1, 0)
            store_f(PAIRS - 1, 1, tail=True)
            load_last_rows(LAYERS)
            for k in range(2):
                sp.wait_ge(f_stored[k], 48 * PAIRS)
                sp.wait_ge(out_done[k], 16 * CT * CPAIRS)

        @block.gpsimd
        def _(pool):
            taken = [0]

            def after(ins):
                taken[0] += 1
                ins.then_inc(consts, 1)
                pool.wait_ge(consts, taken[0])

            after(pool.memset(id_rows[:, 0, :], FAR))
            after(pool.memset(id_rows[:, 1, :], -1))
            pool.memset(id_rows[:, 2, :], 0).then_inc(ids_pad, 1)
            flat = A[:, :, :].rearrange("p t d -> p (t d)").bitcast(I32)
            pool.memset(flat[:, EDGES:TILES * P], FAR).then_inc(bc_pad, 1)
            pool.memset(zeros[:, :], 0.0).then_inc(zero_tile, 1)
            after(pool.memset(ident[:, :], 0.0))
            after(pool.affine_select(out=ident[:, :], in_=ident[:, :], compare_op=ALU.not_equal, fill=1.0, base=0,
                                     pattern=[[-1, P]], channel_multiplier=1))
            after(pool.memset(ones[:, :], 1.0))
            after(pool.memset(eps_c[:, :], EPS))
            for k in range(2):
                after(pool.memset(hp[k][:, :, :], 1.0))
                after(pool.memset(ea[k][:, :, :], 0.0))
            after(pool.memset(gram[:, :], 0.0))
            pool.memset(cross[:, :], 0.0).then_inc(ident_up, 1)
            pool.wait_ge(sel_raw, 1)
            sv = sel_all[:, :].rearrange("j (t e) -> j t e", e=P)
            pool.affine_select(out=sv, in_=sv, compare_op=ALU.is_gt, fill=0.0, base=0,
                               pattern=[[1, TILES], [0, P]], channel_multiplier=-1).then_inc(sel_done, 1)

            def stage(table, ix, c, n):
                pool.tensor_copy(ix[:, :], table[:, ds(c * CT, CT)]).then_inc(staged, 1)
                pool.wait_ge(staged, n)
                plain(pool)

            def gather_src(l, j, k, rows, final):
                if final:
                    pool.wait_ge(tile_sum[k], l * CPAIRS + j)
                else:
                    pool.wait_ge(got_used[k], l * 2 * CPAIRS + j)
                stage(src_i, get_ix[k], 2 * j + k, l * 6 * CPAIRS + 2 * j + k + 1)
                for t in range(CT):
                    pool.indirect_dma_start(got[k][:, t, :], None, rows, bass.IndirectOffsetOnAxis(get_ix[k][:, t:t + 1], 0),
                                            bounds_check=rows.shape[0] - 1, oob_is_err=False).then_inc(src_in[k], 16)

            def gather_dst_and_put(l, j, k, rows, target, limit, done, base):
                if l < LAYERS:
                    pool.wait_ge(got_used[k], l * 2 * CPAIRS + CPAIRS + j)
                else:
                    pool.wait_ge(tile_sum[k], (l + 1) * CPAIRS)
                    pool.wait_ge(got_used[k], l * 2 * CPAIRS + j)
                n = l * 6 * CPAIRS + 2 * CPAIRS + 4 * j + 2 * k
                stage(dst_i, get_ix[k], 2 * j + k, n + 1)
                for t in range(CT):
                    pool.indirect_dma_start(got[k][:, t, :], None, rows, bass.IndirectOffsetOnAxis(get_ix[k][:, t:t + 1], 0),
                                            bounds_check=rows.shape[0] - 1, oob_is_err=False).then_inc(dst_in[k], 16)
                pool.wait_ge(done[k], 16 * CT * (base * CPAIRS + j))
                stage(put_i, put_ix[k], 2 * j + k, n + 2)
                pool.wait_ge(tot_up[k], l * CPAIRS + j + 1)
                plain(pool)
                for t in range(CT):
                    pool.indirect_dma_start(target, bass.IndirectOffsetOnAxis(put_ix[k][:, t:t + 1], 0), tot[k][:, t, :], None,
                                            bounds_check=limit - 1, oob_is_err=False).then_inc(done[k], 16)

            def relu_pair(n, grams):
                for k in range(2):
                    pool.wait_ge(h_bias[k], n + 1)
                    pool.wait_ge(gram_up[k], n + PAIRS if grams else LAYERS * PAIRS)
                    pool.wait_ge(stored[k], 16 * n)
                    plain(pool)
                    pool.tensor_scalar(hp[k][:, :, 0:D], hsum[k][:, :, :], 0.0, None, ALU.max).then_inc(h_up[k], 1)

            pool.wait_ge(tables, 1)
            pool.wait_ge(zeroed, 16 * (ZPARTS + (ZREST > 0)))
            for l in range(LAYERS):
                for k in range(2):
                    if l:
                        pool.wait_ge(stored[k], 16 * PAIRS * l)
                for j in steps(pool, CPAIRS):
                    for k in range(2):
                        gather_src(l, j, k, H_flat[l], False)
                for j in steps(pool, CPAIRS):
                    for k in range(2):
                        gather_dst_and_put(l, j, k, H_flat[l], AGG_flat, NODES, put_done, l)
                for i in steps(pool, PAIRS):
                    relu_pair(l * PAIRS + i, l < LAYERS - 1)

            def normalize(i, k, half):
                pool.wait_ge(f_norm[k], 2 * i + half + 1)
                src_t, dst_t, up = ((fy[k], fx2[k], f_x2[k]), (fs[k], fo[k], f_o[k]))[half]
                if half == 0:
                    pool.wait_ge(f_s[k], i)
                    pool.wait_ge(f_x2T[k], i)
                else:
                    pool.wait_ge(f_stored[k], 48 * i)
                plain(pool)
                for r in range(R):
                    last = pool.tensor_scalar(dst_t[:, r, :], src_t[:, r, :], fstd[k][:, half, r:r + 1], fnm[k][:, half, r:r + 1],
                                              ALU.mult, ALU.add)
                last.then_inc(up, 1)

            normalize(0, 0, 0)
            for i in steps(pool, PAIRS - 1):
                normalize(i, 1, 0)
                normalize(i, 0, 1)
                normalize(i + 1, 0, 0)
                normalize(i, 1, 1)
            normalize(PAIRS - 1, 1, 0)
            normalize(PAIRS - 1, 0, 1)
            normalize(PAIRS - 1, 1, 1)

            for k in range(2):
                pool.wait_ge(f_stored[k], 48 * PAIRS)
            for j in steps(pool, CPAIRS):
                for k in range(2):
                    gather_src(LAYERS, j, k, GR_flat, True)
            for j in steps(pool, CPAIRS):
                for k in range(2):
                    gather_dst_and_put(LAYERS, j, k, SR_flat, out, NODES, out_done, 0)

        @block.vector
        def _(dve):
            taken = [0]

            def after(ins):
                ins.then_inc(dve_step, 1)
                taken[0] += 1
                dve.wait_ge(dve_step, taken[0])

            dve.wait_ge(ids_in, 96)
            for slot, row in ((0, 0), (2, 3)):
                after(dve.tensor_copy(id_float[:, row, :], id_rows[:, slot, :]))
            after(dve.tensor_copy(same_next[:, :], id_rows[:, 1, :]))
            after(dve.tensor_tensor(same_next[:, :], same_next[:, :], id_float[:, 0, :], ALU.is_equal))
            after(dve.scalar_tensor_tensor(id_float[:, 1, :], same_next[:, :], float(FAR), id_float[:, 0, :], ALU.mult, ALU.add))
            dve.tensor_scalar(id_float[:, 2, :], id_float[:, 1, :], float(NODES), None, ALU.is_lt).then_inc(ids_done, 1)
            dve.wait_ge(ids_T, 4)
            after(dve.tensor_copy(dst_c[:, :], psZ[:, 0:TILES]))
            after(dve.tensor_scalar(dst_i[:, :], dst_c[:, :], float(NODES - 1), None, ALU.min))
            after(dve.tensor_copy(put_i[:, :], psZ[:, 128:128 + TILES]))
            after(dve.tensor_copy(rep_c[:, :], psZ[:, 256:256 + TILES]))
            after(dve.tensor_copy(src_i[:, :], psZ[:, 384:384 + TILES]))
            dve.wait_ge(bc_in, 16)
            flat = A[:, :, :].rearrange("p t d -> p (t d)").bitcast(I32)
            dve.tensor_scalar(sel_all[:, :], flat[0:TILES, :], id_float[:, 0, P - 1:P], None, ALU.is_equal).then_inc(sel_raw, 1)
            with dve.Fori(0, TILES // 2) as t:
                for u in range(2):
                    dve.tensor_scalar(eq_all[:, ds(t * 2 * P + u * P, P)], flat[:, ds(t * 2 * P + u * P, P)],
                                      dst_c[:, ds(2 * t + u, 1)], None, ALU.is_equal)
            dve.wait_ge(wcT_up, 1)
            dve.tensor_copy(wcT[:, :], psG[:, 0:D]).then_inc(tables, 1)

            def add_gram(n):
                dve.wait_ge(gram_up[1], n + 1)
                dve.wait_ge(gram_add, n)
                dve.tensor_tensor(gram[:, :], gram[:, :], psG[:, 0:D + 1], ALU.add).then_inc(gram_add, 1)

            dve.wait_ge(ident_up, 1)
            for i in steps(dve, PAIRS):
                add_gram(i)

            def make_msg(l, j, k, last=False):
                n = l * CPAIRS + j
                dve.wait_ge(src_in[k], 16 * CT * (n + 1))
                dve.wait_ge(ea_in[k], 16 * (n + 1))
                if last:
                    dve.wait_ge(ea_tail_in, 16 * (l + 1))
                dve.wait_ge(tile_sum[k], n)
                dve.tensor_tensor(msg[k][:, :, :], got[k][:, :, :], ea[k][:, :, :], ALU.add).then_inc(got_used[k], 1)
                dve.wait_ge(got_used[k], l * 2 * CPAIRS + j + 1)
                dve.tensor_scalar(msg[k][:, :, :], msg[k][:, :, :], 0.0, None, ALU.max).then_inc(msg_up[k], 1)

            def make_total(l, j, k, done, base):
                dve.wait_ge(carry_sum[k], l * CPAIRS + j + 1)
                dve.wait_ge(done[k], 16 * CT * (base * CPAIRS + j))
                for b, (lo, hi) in enumerate(HALVES):
                    ins = dve.tensor_tensor(tot[k][:, lo:hi, :], A[:, ds((2 * j + k) * CT + lo, hi - lo), :],
                                            psU[:, 2 * k + b, 0:(hi - lo) * D].rearrange("p (t d) -> p t d", d=D), ALU.add)
                return ins

            def make_mix(l, j, k):
                n = l * CPAIRS + j
                dve.wait_ge(dst_in[k], 16 * CT * (n + 1))
                dve.tensor_scalar(got[k][:, :, :], got[k][:, :, :], self_w[:, 0:1], None, ALU.mult).then_inc(got_scaled[k], 1)
                dve.wait_ge(got_scaled[k], n + 1)
                dve.wait_ge(tot_up[k], n + 1)
                dve.scalar_tensor_tensor(mix[k][:, :, 0:D], tot[k][:, :, :], 0.5, got[k][:, :, :], ALU.mult, ALU.add).then_inc(got_used[k], 1)
                dve.wait_ge(got_used[k], l * 2 * CPAIRS + CPAIRS + j + 1)
                rep = rep_c[:, ds((2 * j + k) * CT, CT)]
                dve.tensor_tensor(mix[k][:, :, 0:D], mix[k][:, :, 0:D], rep.unsqueeze(2).to_broadcast([P, CT, D]), ALU.mult).then_inc(mix_up[k], 1)
                dve.tensor_copy(mix[k][:, :, D:D + 1], rep.unsqueeze(2)).then_inc(mix_up[k], 1)
                dve.wait_ge(cross_sum[k], n + 1)
                dve.wait_ge(cross_add, 2 * n + k)
                dve.tensor_tensor(cross[:, :], cross[:, :], psH[0][:, 0:D + 1], ALU.add).then_inc(cross_add, 1)

            def sum_z(n):
                for k in range(2):
                    dve.wait_ge(rows_in[k], 32 * (n + 1))
                    dve.wait_ge(z_T[k], n)
                    dve.scalar_tensor_tensor(z[k][:, :], hrow[k][:, :], self_w[:, 0:1], arow[k][:, :], ALU.mult, ALU.add).then_inc(z_up[k], 1)

            def bias_pair(n):
                for k in range(2):
                    dve.wait_ge(h_sum[k], n + 1)
                    dve.wait_ge(h_up[k], n)
                    dve.tensor_tensor(hsum[k][:, :, :], psH[k][:, :].rearrange("p (r d) -> p r d", d=D),
                                      b2_bc[:, :, :].to_broadcast([P, R, D]), ALU.add).then_inc(h_bias[k], 1)

            for l in range(LAYERS):
                done = [0]

                def step(ins):
                    ins.then_inc(bn_step, 1)
                    done[0] += 1
                    dve.wait_ge(bn_step, l * BN_STEPS + done[0])

                dve.wait_ge(weights_in, 16 * BATCH_DMAS * (l + 1))
                step(dve.tensor_scalar(self_w[:, 0:1], eps_in[:, :], 1.0, None, ALU.add))
                step(dve.tensor_tensor(self_w[:, 1:2], self_w[:, 0:1], self_w[:, 0:1], ALU.mult))
                for j in steps(dve, CPAIRS - 1):
                    for k in range(2):
                        make_msg(l, j, k)
                make_msg(l, CPAIRS - 1, 0)
                make_msg(l, CPAIRS - 1, 1, last=True)
                for j in steps(dve, CPAIRS):
                    for k in range(2):
                        make_total(l, j, k, put_done, l).then_inc(tot_up[k], 1)
                        make_mix(l, j, k)
                dve.wait_ge(cross_add, 2 * CPAIRS * (l + 1))
                dve.wait_ge(gram_add, PAIRS * (l + 1))
                step(dve.scalar_tensor_tensor(zz[:, :], gram[:, 0:D], self_w[:, 1:2], cross[:, 0:D], ALU.mult, ALU.add))
                step(dve.scalar_tensor_tensor(zmean[:, :], gram[:, D:D + 1], self_w[:, 0:1], cross[:, D:D + 1], ALU.mult, ALU.add))
                dve.wait_ge(cross_T, l + 1)
                step(dve.tensor_tensor(zz[:, :], zz[:, :], psZ[:, 0:D], ALU.add))
                step(dve.tensor_scalar(zmean[:, :], zmean[:, :], INV_N, None, ALU.mult))
                step(dve.memset(gram[:, :], 0.0))
                step(dve.memset(cross[:, :], 0.0))
                dve.tensor_scalar(zz[:, :], zz[:, :], INV_N, None, ALU.mult).then_inc(zz_up, 1)
                dve.wait_ge(zzw, l + 1)
                dve.tensor_tensor(zw[:, :], w1[:, :], psZ[:, 0:2 * D], ALU.mult).then_inc(zw_up, 1)
                dve.wait_ge(bn_sums, l + 1)
                step(dve.tensor_copy(bn_mu[:, :], psG[:, 2:4]))
                step(dve.tensor_tensor(bn_sq[:, :], bn_mu[:, :], bn_mu[:, :], ALU.mult))
                step(dve.tensor_tensor(bn_var[:, :], psG[:, 0:2], bn_sq[:, :], ALU.subtract))
                dve.tensor_scalar(bn_var[:, :], bn_var[:, :], 0.0, EPS, ALU.max, ALU.add).then_inc(bn_var_up, 1)
                dve.wait_ge(bn_std_up, l + 1)
                step(dve.reciprocal(bn_scale[:, :], bn_std[:, :]))
                step(dve.tensor_tensor(bn_scale[:, :], bn_scale[:, :], bn_in[:, 1, :], ALU.mult))
                step(dve.tensor_tensor(bn_mu[:, :], bn_mu[:, :], bn_in[:, 0, :], ALU.add))
                step(dve.tensor_tensor(bn_mu[:, :], bn_in[:, 0, :], bn_mu[:, :], ALU.subtract))
                step(dve.tensor_tensor(bn_mu[:, :], bn_mu[:, :], bn_scale[:, :], ALU.mult))
                dve.tensor_tensor(bn_bias[:, :], bn_mu[:, :], bn_in[:, 2, :], ALU.add).then_inc(bn_up, 1)
                assert done[0] == BN_STEPS
                sum_z(l * PAIRS)
                for i in steps(dve, PAIRS - 1):
                    sum_z(l * PAIRS + i + 1)
                    bias_pair(l * PAIRS + i)
                    if l < LAYERS - 1:
                        add_gram((l + 1) * PAIRS + i)
                bias_pair(l * PAIRS + PAIRS - 1)
                if l < LAYERS - 1:
                    add_gram((l + 1) * PAIRS + PAIRS - 1)

            def layer_norm(i, k, half, src_t):
                n = 2 * i + half
                for r in range(R):
                    last = dve.bn_stats(fstat[k][:, half, r, :], src_t[:, r, :])
                last.then_inc(f_stat[k], 1)
                dve.wait_ge(f_stat[k], n + 1)
                dve.wait_ge((f_x2[k], f_o[k])[half], i)
                plain(dve)
                for r in range(R):
                    last = dve.bn_aggr(fmv[k][:, half, r, :], fstat[k][:, half, r, :])
                last.then_inc(f_var[k], 1)
                dve.wait_ge(f_std[k], n + 1)
                dve.reciprocal(fstd[k][:, half, :], fstd[k][:, half, :]).then_inc(f_rec[k], 1)
                dve.wait_ge(f_rec[k], n + 1)
                dve.scalar_tensor_tensor(fnm[k][:, half, :], fmv[k][:, half, :, 0], -1.0, fstd[k][:, half, :],
                                         ALU.mult, ALU.mult).then_inc(f_norm[k], 1)

            def front(i, k):
                dve.wait_ge(f_lin[k], i)
                for y in (1, 3):
                    dve.wait_ge(f_T[1], 4 * i + 2 * k + y // 2 + 1)
                    dve.tensor_copy(fT[k][:, 4 * y:4 * y + 4, :], psG[:, :].rearrange("p (r d) -> p r d", d=D)).then_inc(f_copied[1], 1)
                dve.wait_ge(f_lin[k], i + 1)
                dve.wait_ge(f_x2[k], i)
                dve.tensor_tensor(fy[k][:, :, :], psU[:, k, :].rearrange("p (r d) -> p r d", d=D), fh[k][0], ALU.add).then_inc(f_y[k], 1)
                dve.wait_ge(f_y[k], i + 1)
                dve.tensor_tensor(fy[k][:, :, :], fy[k][:, :, :], linb_bc[:, :, :].to_broadcast([P, R, D]), ALU.add).then_inc(f_bias[k], 1)
                dve.wait_ge(f_bias[k], i + 1)
                layer_norm(i, k, 0, fy[k])

            def back(i, k):
                dve.wait_ge(f_w[k], i + 1)
                dve.wait_ge(f_stored[k], 48 * i)
                dve.tensor_tensor(fs[k], psH[k][:, :].rearrange("p (r d) -> p r d", d=D), fx2[k], ALU.add).then_inc(f_s[k], 1)
                dve.wait_ge(f_s[k], i + 1)
                layer_norm(i, k, 1, fs[k])

            front(0, 0)
            for i in steps(dve, PAIRS - 1):
                front(i, 1)
                back(i, 0)
                front(i + 1, 0)
                back(i, 1)
            front(PAIRS - 1, 1)
            back(PAIRS - 1, 0)
            back(PAIRS - 1, 1)

            for j in steps(dve, CPAIRS):
                for k in range(2):
                    n = 2 * j + k
                    make_total(LAYERS, j, k, out_done, 0).then_inc(e_y, 1)
                    dve.wait_ge(dst_in[k], 16 * CT * (LAYERS * CPAIRS + j + 1))
                    dve.wait_ge(e_y, 2 * n + 1)
                    dve.tensor_tensor(mix[k][:, :, 0:D], tot[k][:, :, :], got[k][:, :, :], ALU.add).then_inc(got_used[k], 1)
                    dve.wait_ge(got_used[k], 2 * CPAIRS * LAYERS + j + 1)
                    for t in range(CT):
                        last = dve.bn_stats(estat[:, t, :], mix[k][:, t, 0:D])
                    last.then_inc(e_stat, 1)
                    dve.wait_ge(e_stat, n + 1)
                    plain(dve)
                    for t in range(CT):
                        last = dve.bn_aggr(emv[:, t, :], estat[:, t, :])
                    last.then_inc(e_var, 1)
                    dve.wait_ge(e_std, n + 1)
                    dve.reciprocal(estd[:, :], estd[:, :]).then_inc(e_rec, 1)
                    dve.wait_ge(e_rec, n + 1)
                    dve.scalar_tensor_tensor(enm[:, :], emv[:, :, 0], -1.0, estd[:, :], ALU.mult, ALU.mult).then_inc(e_nm, 1)
                    dve.wait_ge(e_nm, n + 1)
                    for t in range(CT):
                        last = dve.tensor_scalar(tot[k][:, t, :], mix[k][:, t, 0:D], estd[:, t:t + 1], enm[:, t:t + 1], ALU.mult, ALU.add)
                    last.then_inc(e_y, 1)
                    dve.wait_ge(e_y, 2 * n + 2)
                    dve.sem_inc(tot_up[k], 1)

        @block.tensor
        def _(pe):
            pe.wait_ge(ident_up, 1)
            pe.wait_ge(ids_done, 1)
            for row in range(4):
                pe.transpose(psZ[:, row * P:row * P + TILES], id_float[:, row, :], ident[0:TILES, 0:TILES]).then_inc(ids_T, 1)
            pe.wait_ge(const_in, 48)
            pe.transpose(psG[:, 0:P], wc_in[:, :], ident[:, :]).then_inc(wcT_up, 1)
            pe.wait_ge(tables, 1)

            def gram_pair(n, ready, tail):
                pe.wait_ge(gram_add, n)
                for k in range(2):
                    if ready is x_in:
                        pe.wait_ge(x_in[k], 16 * (n + 1))
                    else:
                        pe.wait_ge(h_up[k], n - PAIRS + 1)
                    parts = TAIL_P if tail and k == 1 else P
                    for r in range(R):
                        last = pe.matmul(psG[:, 0:D + 1], hp[k][0:parts, r, 0:D], hp[k][0:parts, r, 0:D + 1],
                                         start=k == 0 and r == 0, stop=k == 1 and r == R - 1)
                    last.then_inc(gram_up[k], 1)

            for i in steps(pe, PAIRS - 1):
                gram_pair(i, x_in, False)
            gram_pair(PAIRS - 1, x_in, True)

            def tile_sums(l, j, k, final=False):
                n = l * CPAIRS + j
                if final:
                    pe.wait_ge(src_in[k], 16 * CT * (n + 1))
                else:
                    pe.wait_ge(msg_up[k], n + 1)
                pe.wait_ge(sel_up[k], l * 2 * CPAIRS + j + 1)
                pe.wait_ge(a_up[k], 2 * n)
                rows = got[k] if final else msg[k]
                for t in range(CT):
                    last = pe.matmul(psU[:, 2 * k + t // 4, (t % 4) * D:(t % 4 + 1) * D], sel[k][:, t * P:(t + 1) * P], rows[:, t, :],
                                     start=True, stop=True)
                last.then_inc(tile_sum[k], 1)

            def carry_sums(l, j, k):
                pe.wait_ge(sel_up[k], l * 2 * CPAIRS + CPAIRS + j + 1)
                for t in range(CT):
                    last = pe.matmul(psU[:, 2 * k + t // 4, (t % 4) * D:(t % 4 + 1) * D], sel[k][0:TILES, t * P:(t + 1) * P],
                                     last_rows[:, :], start=True, stop=True)
                last.then_inc(carry_sum[k], 1)

            def cross_sums(l, j, k):
                n = l * CPAIRS + j
                pe.wait_ge(mix_up[k], 2 * (n + 1))
                pe.wait_ge(cross_add, 2 * n + k)
                for t in range(CT):
                    last = pe.matmul(psH[0][:, 0:D + 1], tot[k][:, t, :], mix[k][:, t, 0:D + 1], start=t == 0, stop=t == CT - 1)
                last.then_inc(cross_sum[k], 1)

            def transposes(n, k):
                pe.wait_ge(z_up[k], n + 1)
                pe.wait_ge(zT_up[1 - k], n + k)
                for r in range(R):
                    last = pe.transpose(psZ[:, r * P:(r + 1) * P], z[k][:, r * D:(r + 1) * D], ident[:, :])
                last.then_inc(z_T[k], 1)

            def up(n, k):
                pe.wait_ge(zT_up[k], n + 1)
                for c in range(2):
                    pe.wait_ge(v_up[k], 2 * n + c if c == 0 else 2 * n)
                    pe.matmul(psU[:, 2 * k + c, :], w1[:, c * D:(c + 1) * D], zT[k][:, :], start=True, stop=True).then_inc(u_up[k], 1)

            def down(n, k):
                pe.wait_ge(v_up[k], 2 * n + 2)
                pe.wait_ge(h_bias[k], n)
                for r in range(R):
                    for c in range(2):
                        last = pe.matmul(psH[k][:, r * D:(r + 1) * D], vT[k][:, c, r * P:(r + 1) * P], w2[:, c, :],
                                         start=c == 0, stop=c == 1)
                last.then_inc(h_sum[k], 1)

            for l in range(LAYERS):
                for j in steps(pe, CPAIRS):
                    for k in range(2):
                        tile_sums(l, j, k)
                pe.wait_ge(last_in, 16 * (l + 1))
                for k in range(2):
                    pe.wait_ge(a_up[k], 2 * CPAIRS * (l + 1))
                for j in steps(pe, CPAIRS):
                    for k in range(2):
                        pe.wait_ge(tot_up[k], l * CPAIRS + j)
                        carry_sums(l, j, k)
                        cross_sums(l, j, k)
                pe.wait_ge(cross_add, 2 * CPAIRS * (l + 1))
                pe.transpose(psZ[:, 0:P], cross[:, 0:D], ident[:, :]).then_inc(cross_T, 1)
                pe.wait_ge(zz_up, l + 1)
                pe.matmul(psZ[:, 0:2 * D], zz[:, :], w1[:, :], start=True, stop=True).then_inc(zzw, 1)
                pe.wait_ge(zw_up, l + 1)
                for c in range(2):
                    pe.matmul(psG[:, c:c + 1], zw[:, c * D:(c + 1) * D], ones[:, :], start=True, stop=True)
                for c in range(2):
                    last = pe.matmul(psG[:, 2 + c:3 + c], w1[:, c * D:(c + 1) * D], zmean[:, :], start=True, stop=True)
                last.then_inc(bn_sums, 1)
                n = l * PAIRS
                transposes(n, 0)
                transposes(n, 1)
                pe.wait_ge(bn_up, l + 1)
                for i in steps(pe, PAIRS - 1):
                    m = l * PAIRS + i
                    up(m, 0)
                    transposes(m + 1, 0)
                    up(m, 1)
                    transposes(m + 1, 1)
                    down(m, 0)
                    down(m, 1)
                    if l < LAYERS - 1:
                        gram_pair(m + PAIRS, h_up, False)
                m = l * PAIRS + PAIRS - 1
                up(m, 0)
                up(m, 1)
                down(m, 0)
                down(m, 1)
                if l < LAYERS - 1:
                    gram_pair(m + PAIRS, h_up, True)

            def front(i, k):
                pe.wait_ge(f_in[k], 64 * (i + 1))
                for y in range(LAYERS + 1):
                    bank = (psZ, psG)[y % 2]
                    pe.wait_ge(f_copied[y % 2], 4 * i + 2 * k + y // 2)
                    for r in range(R):
                        last = pe.transpose(bank[:, r * P:(r + 1) * P], fh[k][y][:, r, :], ident[:, :])
                    last.then_inc(f_T[y % 2], 1)
                for half in range(2):
                    pe.wait_ge(f_copied[half], 4 * i + 2 * k + 2)
                pe.wait_ge(f_y[k], i)
                for r in range(R):
                    for y in range(LAYERS + 1):
                        last = pe.matmul(psU[:, k, r * D:(r + 1) * D], fT[k][:, 4 * y + r, :], lin[:, y, :],
                                         start=y == 0, stop=y == LAYERS)
                last.then_inc(f_lin[k], 1)

            def back(i, k):
                pe.wait_ge(f_x2[k], i + 1)
                pe.wait_ge(f_x2c[k], i)
                for r in range(R):
                    last = pe.transpose(psU[:, 2 + k, r * P:(r + 1) * P], fx2[k][:, r, :], ident[:, :])
                last.then_inc(f_x2T[k], 1)
                pe.wait_ge(f_x2c[k], i + 1)
                pe.wait_ge(f_s[k], i)
                pe.wait_ge(f_g[k], i)
                for r in range(R):
                    last = pe.matmul(psH[k][:, r * D:(r + 1) * D], fx2T[k][:, r * P:(r + 1) * P], wcT[:, :], start=True, stop=True)
                last.then_inc(f_w[k], 1)

            front(0, 0)
            for i in steps(pe, PAIRS - 1):
                front(i, 1)
                back(i, 0)
                front(i + 1, 0)
                back(i, 1)
            front(PAIRS - 1, 1)
            back(PAIRS - 1, 0)
            back(PAIRS - 1, 1)

            for j in steps(pe, CPAIRS):
                for k in range(2):
                    tile_sums(LAYERS, j, k, final=True)
            pe.wait_ge(last_in, 16 * (LAYERS + 1))
            for k in range(2):
                pe.wait_ge(a_up[k], 2 * CPAIRS * (LAYERS + 1))
            for j in steps(pe, CPAIRS):
                for k in range(2):
                    pe.wait_ge(tot_up[k], LAYERS * CPAIRS + j)
                    carry_sums(LAYERS, j, k)

        @block.scalar
        def _(act):
            def edge_chunk(l, j, k):
                n = l * CPAIRS + j
                c = (2 * j + k) * CT
                act.wait_ge(tile_sum[k], n)
                act.wait_ge(carry_sum[k], l * CPAIRS)
                act.copy(sel[k][:, :], eq_all[:, ds(c * P, CT * P)]).then_inc(sel_up[k], 1)
                act.wait_ge(tile_sum[k], n + 1)
                for b, (lo, hi) in enumerate(HALVES):
                    act.copy(A[:, ds(c + lo, hi - lo), :], psU[:, 2 * k + b, 0:(hi - lo) * D].rearrange("p (t d) -> p t d", d=D)).then_inc(a_up[k], 1)

            def carry_chunk(l, j, k):
                act.wait_ge(tile_sum[k], (l + 1) * CPAIRS)
                act.wait_ge(carry_sum[k], l * CPAIRS + j)
                act.copy(sel[k][0:TILES, :], sel_all[:, ds((2 * j + k) * CT * P, CT * P)]).then_inc(sel_up[k], 1)

            def copy_z(n, k):
                act.wait_ge(z_T[k], n + 1)
                act.wait_ge(u_up[k], 2 * n)
                act.copy(zT[k][:, :], psZ[:, :]).then_inc(zT_up[k], 1)

            def relu_u(n, k):
                for c in range(2):
                    act.wait_ge(u_up[k], 2 * n + c + 1)
                    act.wait_ge(h_sum[k], n)
                    act.activation(vT[k][:, c, :], psU[:, 2 * k + c, :], ACT.Relu, bias=bn_bias[:, c:c + 1],
                                   scale=bn_scale[:, c:c + 1]).then_inc(v_up[k], 1)

            act.wait_ge(tables, 1)
            act.wait_ge(sel_done, 1)
            for l in range(LAYERS):
                for j in steps(act, CPAIRS):
                    for k in range(2):
                        edge_chunk(l, j, k)
                for j in steps(act, CPAIRS):
                    for k in range(2):
                        carry_chunk(l, j, k)
                act.wait_ge(bn_var_up, l + 1)
                act.activation(bn_std[:, :], bn_var[:, :], ACT.Sqrt).then_inc(bn_std_up, 1)
                n = l * PAIRS
                copy_z(n, 0)
                copy_z(n, 1)
                act.wait_ge(bn_up, l + 1)
                for i in steps(act, PAIRS - 1):
                    m = l * PAIRS + i
                    for k in range(2):
                        relu_u(m, k)
                        copy_z(m + 1, k)
                for k in range(2):
                    relu_u(l * PAIRS + PAIRS - 1, k)

            def root(i, k, half):
                act.wait_ge(f_var[k], 2 * i + half + 1)
                act.activation(fstd[k][:, half, :], fmv[k][:, half, :, 1], ACT.Sqrt, bias=eps_c[:, :]).then_inc(f_std[k], 1)

            def front(i, k):
                act.wait_ge(f_lin[k], i)
                for y in (0, 2):
                    act.wait_ge(f_T[0], 4 * i + 2 * k + y // 2 + 1)
                    act.copy(fT[k][:, 4 * y:4 * y + 4, :], psZ[:, :].rearrange("p (r d) -> p r d", d=D)).then_inc(f_copied[0], 1)
                root(i, k, 0)

            def back(i, k):
                act.wait_ge(f_x2T[k], i + 1)
                act.wait_ge(f_w[k], i)
                act.copy(fx2T[k][:, :], psU[:, 2 + k, :]).then_inc(f_x2c[k], 1)
                act.wait_ge(f_w[k], i + 1)
                act.wait_ge(f_s[k], i + 1)
                act.wait_ge(f_stored[k], 48 * i)
                act.copy(fg[k][:, :], psH[k][:, :]).then_inc(f_g[k], 1)
                root(i, k, 1)

            front(0, 0)
            for i in steps(act, PAIRS - 1):
                front(i, 1)
                back(i, 0)
                front(i + 1, 0)
                back(i, 1)
            front(PAIRS - 1, 1)
            back(PAIRS - 1, 0)
            back(PAIRS - 1, 1)

            for j in steps(act, CPAIRS):
                for k in range(2):
                    edge_chunk(LAYERS, j, k)
            for j in steps(act, CPAIRS):
                for k in range(2):
                    carry_chunk(LAYERS, j, k)
                    act.wait_ge(e_var, 2 * j + k + 1)
                    act.activation(estd[:, :], emv[:, :, 1], ACT.Sqrt, bias=eps_c[:, :]).then_inc(e_std, 1)


_INS = ["x", "src", "dst", "edge_attr_128", "L0_gnn_eps", "L0_gnn_W1", "L0_gnn_b1", "L0_gnn_gamma", "L0_gnn_beta",
        "L0_gnn_W2", "L0_gnn_b2", "L0_gnn_lin_w", "L0_gnn_lin_b", "L1_gnn_W"]


def kernel(**inputs):
    import numpy as _np
    import concourse.bacc as _bacc
    from concourse import mybir as _mybir
    from concourse.bass_utils import run_bass_kernel_spmd as _run

    nc = _bacc.Bacc("TRN2", target_bir_lowering=False, num_devices=1)
    arrays, args = {}, []
    for name in _INS:
        a = _np.ascontiguousarray(inputs[name])
        arrays[f"in_{name}"] = a
        args.append(nc.dram_tensor(f"in_{name}", a.shape, _mybir.dt.from_np(a.dtype), kind="ExternalInput").ap())
    result = nc.dram_tensor("out_rows", (NODES, D), F32, kind="ExternalOutput").ap()
    gnn_kernel(nc, *args, result)
    r = _run(nc, [arrays], core_ids=[0])
    return r.results[0]["out_rows"]
```

```python
from contextlib import ExitStack

import concourse.bass as bass
from concourse import mybir

F32 = mybir.dt.float32
I32 = mybir.dt.int32
BF16 = mybir.dt.bfloat16
ALU = mybir.AluOpType
ACT = mybir.ActivationFunctionType

P = 128
D = 128
NODES = 50000
EDGES = 12500
LAYERS = 3
R = 4
GROUP = P * R
GROUPS = -(-NODES // GROUP)
PAIRS = GROUPS // 2
ROWS = GROUPS * GROUP
TAIL_P = (NODES - (GROUPS - 1) * GROUP) // R
TILES = -(-EDGES // P)
TAIL_E = EDGES - (TILES - 1) * P
CT = 7
CPAIRS = TILES // CT // 2
FAR = 1 << 20
INV_N = 1.0 / NODES
EPS = 1e-5
ZCOLS = 2000
ZPARTS = ROWS * D // P // ZCOLS
ZREST = ROWS * D // P - ZPARTS * ZCOLS
HALVES = ((0, 4), (4, 7))
BATCH_DMAS = 7
XS = GROUPS // (2 * CPAIRS)
BN_STEPS = 16


def steps(eng, end):
    yield 0
    with eng.Fori(1, end) as i:
        yield i


def group_steps(eng, stages):
    def step(i, k):
        for do, lead in stages:
            t = k + lead
            if not isinstance(i, int) or 0 <= 2 * i + t < GROUPS:
                do(i + t // 2, t % 2)

    head, tail = 3, PAIRS - 1
    step(-1, 1)
    for s in range(2 * head):
        step(s // 2, s % 2)
    with eng.Fori(head, tail) as i:
        step(i, 0)
        step(i, 1)
    for s in range(2 * tail, 2 * tail + 6):
        step(s // 2, s % 2)


def gnn_kernel(nc, x, src, dst, edge_attr, eps, W1, b1, gamma, beta, W2, b2, lin_w, lin_b, Wc, out):
    ds = bass.ds
    H = [None] + [nc.dram_tensor(f"h{l}_rows", [GROUPS, P, R * D], F32).ap() for l in range(1, LAYERS + 1)]
    AGG = nc.dram_tensor("agg_rows", [GROUPS, P, R * D], F32).ap()
    GR = nc.dram_tensor("g_rows", [GROUPS, P, R * D], F32).ap()
    SR = nc.dram_tensor("s_rows", [GROUPS, P, R * D], F32).ap()
    LAST = nc.dram_tensor("last_rows_dram", [1, TILES, D], F32).ap()
    H_flat = [x] + [h.rearrange("g p (r d) -> (g p r) d", r=R) for h in H[1:]]
    AGG_flat = AGG.rearrange("g p (r d) -> (g p r) d", r=R)
    GR_flat = GR.rearrange("g p (r d) -> (g p r) d", r=R)
    SR_flat = SR.rearrange("g p (r d) -> (g p r) d", r=R)
    BODY = (GROUPS - 1) * GROUP
    x_groups = x[0:BODY, :].rearrange("(g p r) d -> g p r d", p=P, r=R)
    x_tail = x[BODY:NODES, :].rearrange("(p r) d -> p r d", r=R)
    out_groups = out[0:BODY, :].rearrange("(g p r) d -> g p (r d)", p=P, r=R)
    out_tail = out[BODY:NODES, :].rearrange("(p r) d -> p (r d)", r=R)
    ea_tiles = edge_attr[0:(TILES - 1) * P, :].rearrange("(t p) d -> p t d", p=P)

    with ExitStack() as ctx:
        def sb(name, shape, dt=F32):
            return ctx.enter_context(nc.sbuf_tensor(name, shape, dt))

        def sem(name):
            return ctx.enter_context(nc.semaphore(name))

        def sems(name, n=2):
            return [sem(f"{name}{k}") for k in range(n)]

        def bufs(name, shape, dt=F32):
            return [sb(f"{name}{k}", shape, dt) for k in range(2)]

        ident = sb("ident", [P, P])
        eq_all = sb("eq_all", [P, TILES * P], BF16)
        sel_all = sb("sel_all", [TILES, TILES * P], BF16)
        zeros = sb("zeros", [P, ZCOLS])
        id_rows = sb("id_rows", [TILES, 3, P], I32)
        id_float = sb("id_float", [TILES, 4, P])
        same_next = sb("same_next", [TILES, P])
        dst_c = sb("dst_c", [P, TILES])
        rep_c = sb("rep_c", [P, TILES])
        src_i = sb("src_i", [P, TILES], I32)
        dst_i = sb("dst_i", [P, TILES], I32)
        put_i = sb("put_i", [P, TILES], I32)
        w1 = sb("w1", [P, 2 * D])
        w2 = sb("w2", [P, 2, D])
        lin = sb("lin", [P, LAYERS + 1, D])
        wc_in = sb("wc_in", [P, D])
        wcT = sb("wcT", [P, D])
        b2_bc = sb("b2_bc", [P, 1, D])
        linb_bc = sb("linb_bc", [P, 1, D])
        bn_in = sb("bn_in", [P, 3, 2])
        eps_in = sb("eps_in", [P, 1])
        self_w = sb("self_w", [P, 2])
        gram = sb("gram", [P, D + 1])
        cross = sb("cross", [P, D + 1])
        zz = sb("zz", [P, D])
        zmean = sb("zmean", [P, 1])
        zw = sb("zw", [P, 2 * D])
        ones = sb("ones", [P, 1])
        eps_c = sb("eps_c", [P, 1])
        bn_mu = sb("bn_mu", [P, 2])
        bn_sq = sb("bn_sq", [P, 2])
        bn_var = sb("bn_var", [P, 2])
        bn_std = sb("bn_std", [P, 2])
        bn_scale = sb("bn_scale", [P, 2])
        bn_bias = sb("bn_bias", [P, 2])
        A = sb("A", [P, TILES, D])
        last_rows = sb("last_rows", [TILES, D])
        got = bufs("got", [P, CT, D])
        ea = bufs("ea", [P, CT, D])
        msg = bufs("msg", [P, CT, D])
        sel = bufs("sel", [P, CT * P])
        tot = bufs("tot", [P, CT, D])
        mix = bufs("mix", [P, CT, D + 2])
        get_ix = bufs("get_ix", [P, CT], I32)
        put_ix = bufs("put_ix", [P, CT], I32)
        estat = sb("estat", [P, CT, 6])
        emv = sb("emv", [P, CT, 2])
        estd = sb("estd", [P, CT])
        enm = sb("enm", [P, CT])
        hrow = bufs("hrow", [P, R * D])
        arow = bufs("arow", [P, R * D])
        z = bufs("z", [P, R * D])
        zT = bufs("zT", [P, R * D])
        vT = bufs("vT", [P, 2, R * D])
        hsum = bufs("hsum", [P, R, D])
        hp = bufs("hp", [P, R, D + 4])
        xg = [t[:, 0:R, :] for t in hp + mix] + [sb(f"xg{q}", [P, R, D + 2])[:, :, :] for q in range(4, XS)]
        fh = [[A[:, (4 * (4 * k + y)):(4 * (4 * k + y)) + 4, :] for y in range(4)] for k in range(2)]
        fT = [A[:, 32 + 16 * k:48 + 16 * k, :] for k in range(2)]
        fstat = [sb(f"fstat{k}", [P, 2, R, 6]) for k in range(2)]
        fmv = [sb(f"fmv{k}", [P, 2, R, 2]) for k in range(2)]
        fstd = [sb(f"fstd{k}", [P, 2, R]) for k in range(2)]
        fnm = [sb(f"fnm{k}", [P, 2, R]) for k in range(2)]
        fy = hsum
        fx2 = [t[:, 0:R, :] for t in msg]
        fx2T = z
        fg = hrow
        fs = [t[:, 0:R, :] for t in got]
        fo = [t[:, 0:R, :] for t in ea]

        psZ = ctx.enter_context(nc.psum_tensor("psZ", [P, 512], F32))
        psU = ctx.enter_context(nc.psum_tensor("psU", [P, 4, 512], F32))
        psH = [ctx.enter_context(nc.psum_tensor(f"psH{k}", [P, 512], F32)) for k in range(2)]
        psG = ctx.enter_context(nc.psum_tensor("psG", [P, 512], F32))

        ids_in = sem("ids_in"); ids_pad = sem("ids_pad"); consts = sem("consts"); passed = sem("passed"); ident_up = sem("ident_up")
        const_in = sem("const_in"); bc_in = sem("bc_in"); zeroed = sem("zeroed"); zero_tile = sem("zero_tile")
        ids_done = sem("ids_done"); ids_T = sem("ids_T"); sel_raw = sem("sel_raw"); sel_done = sem("sel_done")
        tables = sem("tables"); wcT_up = sem("wcT_up"); dve_step = sem("dve_step"); bc_pad = sem("bc_pad")
        x_in = sems("x_in", XS); x_gram = sem("x_gram"); x_add = sem("x_add")
        weights_in = sem("weights_in"); staged = sem("staged")
        src_in = sems("src_in"); ea_in = sems("ea_in"); ea_tail_in = sem("ea_tail_in")
        msg_up = sems("msg_up"); sel_up = sems("sel_up"); tile_sum = sems("tile_sum"); a_up = sems("a_up")
        last_in = sem("last_in"); last_out = sem("last_out"); carry_sum = sems("carry_sum"); dst_in = sems("dst_in")
        tot_up = sems("tot_up"); put_done = sems("put_done"); mix_up = sems("mix_up"); cross_sum = sems("cross_sum")
        cross_add = sem("cross_add"); got_used = sems("got_used"); got_scaled = sems("got_scaled")
        cross_T = sem("cross_T"); zz_up = sem("zz_up"); zzw = sem("zzw"); zw_up = sem("zw_up"); bn_sums = sem("bn_sums")
        bn_var_up = sem("bn_var_up"); bn_std_up = sem("bn_std_up"); bn_up = sem("bn_up")
        rows_in = sems("rows_in"); z_up = sems("z_up"); z_T = sems("z_T"); zT_up = sems("zT_up")
        u_up = sems("u_up"); v_up = sems("v_up"); h_sum = sems("h_sum"); h_bias = sems("h_bias"); h_up = sems("h_up")
        gram_up = sems("gram_up"); gram_add = sem("gram_add"); stored = sems("stored")
        f_in = sems("f_in"); f_T = sems("f_T"); f_copied = sems("f_copied"); f_lin = sems("f_lin"); f_y = sems("f_y")
        f_stat = sems("f_stat"); f_rec = sems("f_rec"); f_var = sems("f_var"); f_std = sems("f_std"); f_norm = sems("f_norm"); f_norm2 = sems("f_norm2"); f_std2 = sems("f_std2"); f_rec2 = sems("f_rec2"); f_stat2 = sems("f_stat2"); f_var2 = sems("f_var2"); f_x2 = sems("f_x2")
        f_x2T = sems("f_x2T"); f_x2c = sems("f_x2c"); f_w = sems("f_w"); f_g = sems("f_g"); f_s = sems("f_s"); f_o = sems("f_o")
        f_stored = sems("f_stored"); e_y = sem("e_y"); e_stat = sem("e_stat"); e_var = sem("e_var"); e_std = sem("e_std"); e_rec = sem("e_rec"); e_nm = sem("e_nm"); bn_step = sem("bn_step"); out_done = sems("out_done")

        def plain(eng):
            eng.sem_inc(passed, 1)

        block = ctx.enter_context(nc.Block())

        @block.sync
        def _(sp):
            sp.wait_ge(ids_pad, 1)
            whole = (TILES - 1) * P
            for slot, ids in ((0, dst), (2, src)):
                sp.dma_start(id_rows[0:TILES - 1, slot, :], ids[0:whole].rearrange("(t p) -> t p", p=P)).then_inc(ids_in, 16)
                sp.dma_start(id_rows[TILES - 1:TILES, slot, 0:TAIL_E], ids[whole:EDGES].rearrange("(t p) -> t p", t=1)).then_inc(ids_in, 16)
            sp.dma_start(id_rows[0:TILES - 1, 1, :], dst[1:whole + 1].rearrange("(t p) -> t p", p=P)).then_inc(ids_in, 16)
            sp.dma_start(id_rows[TILES - 1:TILES, 1, 0:TAIL_E - 1], dst[whole + 1:EDGES].rearrange("(t p) -> t p", t=1)).then_inc(ids_in, 16)
            sp.wait_ge(bc_pad, 1)
            flat = A[:, :, :].rearrange("p t d -> p (t d)").bitcast(I32)
            sp.dma_start(flat[:, 0:EDGES], dst.partition_broadcast(P)).then_inc(bc_in, 16)
            sp.dma_start(lin[:, :, :], lin_w.rearrange("(y k) d -> k y d", k=D)).then_inc(const_in, 16)
            sp.dma_start(wc_in[:, :], Wc).then_inc(const_in, 16)
            sp.dma_start(linb_bc[:, 0, :], lin_b.partition_broadcast(P)).then_inc(const_in, 16)
            sp.wait_ge(ident_up, 1)

            def load_x(j, k, tail=False):
                c = 2 * j + k
                for q in range(XS):
                    if q == 0:
                        sp.wait_ge(x_gram, c)
                    if tail and q == XS - 1:
                        sp.dma_start(xg[q][0:TAIL_P, :, 0:D], x_tail).then_inc(x_in[q], 16)
                    else:
                        sp.dma_start(xg[q][:, :, 0:D], x_groups[ds(c * XS + q, 1), :, :, :].rearrange("o p r d -> (o p) r d")).then_inc(x_in[q], 16)

            def load_ea(l, j, k, last=False):
                sp.wait_ge(msg_up[k], l * CPAIRS + j)
                c = (2 * j + k) * CT
                if last:
                    sp.dma_start(ea[k][:, 0:CT - 1, :], ea_tiles[:, c:c + CT - 1, :]).then_inc(ea_in[k], 16)
                    sp.dma_start(ea[k][0:TAIL_E, CT - 1, :], edge_attr[(TILES - 1) * P:EDGES, :]).then_inc(ea_tail_in, 16)
                else:
                    sp.dma_start(ea[k][:, :, :], ea_tiles[:, ds(c, CT), :]).then_inc(ea_in[k], 16)

            def load_last_rows(l):
                for k in range(2):
                    sp.wait_ge(a_up[k], 2 * CPAIRS * (l + 1))
                sp.dma_start(LAST, A[P - 1:P, :, :]).then_inc(last_out, 16)
                sp.wait_ge(last_out, 16 * (l + 1))
                sp.dma_start(last_rows[:, :], LAST.rearrange("o t d -> (o t) d")).then_inc(last_in, 16)

            def h_group(y, g, to, done, tail=False):
                if y:
                    sp.dma_start(to, H[y][ds(g, 1), :, :].rearrange("o p (r d) -> (o p) r d", r=R)).then_inc(done, 16)
                elif tail:
                    sp.dma_start(to[0:TAIL_P], x_tail).then_inc(done, 16)
                else:
                    sp.dma_start(to, x_groups[ds(g, 1), :, :, :].rearrange("o p r d -> (o p) r d")).then_inc(done, 16)

            def load_rows(l, n, i, last=False):
                for k in range(2):
                    sp.wait_ge(z_up[k], n)
                    g = 2 * i + k
                    h_group(l, g, hrow[k][:, :].rearrange("p (r d) -> p r d", d=D), rows_in[k], last and k == 1)
                    sp.dma_start(arow[k][:, :], AGG[ds(g, 1), :, :].rearrange("o p n -> (o p) n")).then_inc(rows_in[k], 16)

            def store_pair(l, i):
                n = l * PAIRS + i
                for k in range(2):
                    sp.wait_ge(h_up[k], n + 1)
                    sp.dma_start(H[l + 1][ds(2 * i + k, 1), :, :].rearrange("o p (r d) -> (o p) r d", r=R),
                                 hp[k][:, :, 0:D]).then_inc(stored[k], 16)

            for l in range(LAYERS):
                for k in range(2):
                    if l:
                        sp.wait_ge(stored[k], 16 * PAIRS * l)
                sp.dma_start(w1[:, :], W1[l]).then_inc(weights_in, 16)
                sp.dma_start(w2[:, :, :], W2[l].rearrange("(c k) n -> k c n", c=2)).then_inc(weights_in, 16)
                for row, vec in enumerate((b1, gamma, beta)):
                    with nc.allow_non_contiguous_dma("256 features"):
                        sp.dma_start(bn_in[:, row, :], vec[l].rearrange("(c f) -> f c", c=2)).then_inc(weights_in, 16)
                sp.dma_start(b2_bc[:, 0, :], b2[l].partition_broadcast(P)).then_inc(weights_in, 16)
                sp.dma_start(eps_in[:, :], eps[l:l + 1].partition_broadcast(P)).then_inc(weights_in, 16)
                for j in steps(sp, CPAIRS - 1):
                    for k in range(2):
                        load_ea(l, j, k)
                        if l == 0:
                            load_x(j, k)
                load_ea(l, CPAIRS - 1, 0)
                if l == 0:
                    load_x(CPAIRS - 1, 0)
                load_ea(l, CPAIRS - 1, 1, last=True)
                if l == 0:
                    load_x(CPAIRS - 1, 1, tail=True)
                    sp.wait_ge(zero_tile, 1)
                    agg_parts = AGG.rearrange("g p n -> (g p n)").rearrange("(p n) -> p n", p=P)
                    with sp.Fori(0, ZPARTS) as i:
                        sp.dma_start(agg_parts[:, ds(i * ZCOLS, ZCOLS)], zeros[:, :]).then_inc(zeroed, 16)
                    if ZREST:
                        sp.dma_start(agg_parts[:, ZPARTS * ZCOLS:], zeros[:, 0:ZREST]).then_inc(zeroed, 16)
                load_last_rows(l)
                for k in range(2):
                    sp.wait_ge(put_done[k], 16 * CT * CPAIRS * (l + 1))
                sp.wait_ge(zeroed, 16 * (ZPARTS + (ZREST > 0)))
                load_rows(l, l * PAIRS, 0)
                load_rows(l, l * PAIRS + 1, 1)
                for i in steps(sp, PAIRS - 3):
                    load_rows(l, l * PAIRS + i + 2, i + 2)
                    store_pair(l, i)
                load_rows(l, (l + 1) * PAIRS - 1, PAIRS - 1, last=True)
                store_pair(l, PAIRS - 3)
                store_pair(l, PAIRS - 2)
                store_pair(l, PAIRS - 1)

            for k in range(2):
                sp.wait_ge(stored[k], 16 * PAIRS * LAYERS)

            def load_f(i, k, last=False):
                if not isinstance(i, int) or i:
                    for half in range(2):
                        sp.wait_ge(f_T[half], 4 * i + 2 * k - 2)
                for y in range(LAYERS + 1):
                    h_group(y, 2 * i + k, fh[k][y], f_in[k], last and k == 1)

            def store_f(i, k, tail=False):
                sp.wait_ge(f_g[k], i + 1)
                sp.dma_start(GR[ds(2 * i + k, 1), :, :].rearrange("o p n -> (o p) n"), fg[k][:, :]).then_inc(f_stored[k], 16)
                sp.wait_ge(f_s[k], i + 1)
                sp.dma_start(SR[ds(2 * i + k, 1), :, :].rearrange("o p (r d) -> (o p) r d", r=R), fs[k]).then_inc(f_stored[k], 16)
                sp.wait_ge(f_o[k], i + 1)
                if tail:
                    sp.dma_start(out_tail.rearrange("p (r d) -> p r d", r=R), fo[k][0:TAIL_P]).then_inc(f_stored[k], 16)
                else:
                    sp.dma_start(out_groups[ds(2 * i + k, 1), :, :].rearrange("o p (r d) -> (o p) r d", r=R), fo[k]).then_inc(f_stored[k], 16)

            for i in range(3):
                for k in range(2):
                    load_f(i, k)
            for i in steps(sp, PAIRS - 4):
                for k in range(2):
                    load_f(i + 3, k)
                    store_f(i, k)
            for k in range(2):
                load_f(PAIRS - 1, k, last=True)
                store_f(PAIRS - 4, k)
            for k in range(2):
                store_f(PAIRS - 3, k)
            for k in range(2):
                store_f(PAIRS - 2, k)
            for k in range(2):
                store_f(PAIRS - 1, k, tail=k == 1)
            load_last_rows(LAYERS)
            for k in range(2):
                sp.wait_ge(f_stored[k], 48 * PAIRS)
                sp.wait_ge(out_done[k], 16 * CT * CPAIRS)

        @block.gpsimd
        def _(pool):
            taken = [0]

            def after(ins):
                taken[0] += 1
                ins.then_inc(consts, 1)
                pool.wait_ge(consts, taken[0])

            after(pool.memset(id_rows[:, 0, :], FAR))
            after(pool.memset(id_rows[:, 1, :], -1))
            pool.memset(id_rows[:, 2, :], 0).then_inc(ids_pad, 1)
            flat = A[:, :, :].rearrange("p t d -> p (t d)").bitcast(I32)
            pool.memset(flat[:, EDGES:TILES * P], FAR).then_inc(bc_pad, 1)
            pool.memset(zeros[:, :], 0.0).then_inc(zero_tile, 1)
            after(pool.memset(ident[:, :], 0.0))
            after(pool.affine_select(out=ident[:, :], in_=ident[:, :], compare_op=ALU.not_equal, fill=1.0, base=0,
                                     pattern=[[-1, P]], channel_multiplier=1))
            after(pool.memset(ones[:, :], 1.0))
            after(pool.memset(eps_c[:, :], EPS))
            for k in range(2):
                after(pool.memset(hp[k][:, :, :], 1.0))
                after(pool.memset(mix[k][:, :, :], 1.0))
                after(pool.memset(ea[k][:, :, :], 0.0))
            for q in range(4, XS):
                after(pool.memset(xg[q], 1.0))
            after(pool.memset(gram[:, :], 0.0))
            pool.memset(cross[:, :], 0.0).then_inc(ident_up, 1)
            pool.wait_ge(sel_raw, 1)
            sv = sel_all[:, :].rearrange("j (t e) -> j t e", e=P)
            pool.affine_select(out=sv, in_=sv, compare_op=ALU.is_gt, fill=0.0, base=0,
                               pattern=[[1, TILES], [0, P]], channel_multiplier=-1).then_inc(sel_done, 1)

            def stage(table, ix, c, n):
                pool.tensor_copy(ix[:, :], table[:, ds(c * CT, CT)]).then_inc(staged, 1)
                pool.wait_ge(staged, n)
                plain(pool)

            def gather_src(l, j, k, rows, final):
                if final:
                    pool.wait_ge(tile_sum[k], l * CPAIRS + j)
                else:
                    pool.wait_ge(got_used[k], l * 2 * CPAIRS + j)
                stage(src_i, get_ix[k], 2 * j + k, l * 6 * CPAIRS + 2 * j + k + 1)
                for t in range(CT):
                    pool.indirect_dma_start(got[k][:, t, :], None, rows, bass.IndirectOffsetOnAxis(get_ix[k][:, t:t + 1], 0),
                                            bounds_check=rows.shape[0] - 1, oob_is_err=False).then_inc(src_in[k], 16)

            def gather_dst_and_put(l, j, k, rows, target, limit, done, base):
                if l < LAYERS:
                    pool.wait_ge(got_used[k], l * 2 * CPAIRS + CPAIRS + j)
                else:
                    pool.wait_ge(tile_sum[k], (l + 1) * CPAIRS)
                    pool.wait_ge(got_used[k], l * 2 * CPAIRS + j)
                n = l * 6 * CPAIRS + 2 * CPAIRS + 4 * j + 2 * k
                stage(dst_i, get_ix[k], 2 * j + k, n + 1)
                for t in range(CT):
                    pool.indirect_dma_start(got[k][:, t, :], None, rows, bass.IndirectOffsetOnAxis(get_ix[k][:, t:t + 1], 0),
                                            bounds_check=rows.shape[0] - 1, oob_is_err=False).then_inc(dst_in[k], 16)
                pool.wait_ge(done[k], 16 * CT * (base * CPAIRS + j))
                stage(put_i, put_ix[k], 2 * j + k, n + 2)
                pool.wait_ge(tot_up[k], l * CPAIRS + j + 1)
                plain(pool)
                for t in range(CT):
                    pool.indirect_dma_start(target, bass.IndirectOffsetOnAxis(put_ix[k][:, t:t + 1], 0), tot[k][:, t, :], None,
                                            bounds_check=limit - 1, oob_is_err=False).then_inc(done[k], 16)

            pool.wait_ge(tables, 1)
            for l in range(LAYERS):
                for k in range(2):
                    if l:
                        pool.wait_ge(stored[k], 16 * PAIRS * l)
                for j in steps(pool, CPAIRS):
                    for k in range(2):
                        gather_src(l, j, k, H_flat[l], False)
                if l == 0:
                    pool.wait_ge(zeroed, 16 * (ZPARTS + (ZREST > 0)))
                for j in steps(pool, CPAIRS):
                    for k in range(2):
                        gather_dst_and_put(l, j, k, H_flat[l], AGG_flat, NODES, put_done, l)

            def normalize(i, k, half):
                pool.wait_ge((f_norm, f_norm2)[half][k], i + 1)
                src_t, dst_t, up = ((fy[k], fx2[k], f_x2[k]), (fs[k], fo[k], f_o[k]))[half]
                if half == 0:
                    pool.wait_ge(f_s[k], i)
                    pool.wait_ge(f_x2T[k], i)
                else:
                    pool.wait_ge(f_stored[k], 48 * i)
                plain(pool)
                for r in range(R):
                    last = pool.tensor_scalar(dst_t[:, r, :], src_t[:, r, :], fstd[k][:, half, r:r + 1], fnm[k][:, half, r:r + 1],
                                              ALU.mult, ALU.add)
                last.then_inc(up, 1)

            group_steps(pool, ((lambda i, k: normalize(i, k, 0), -1), (lambda i, k: normalize(i, k, 1), -4)))

            for k in range(2):
                pool.wait_ge(f_stored[k], 48 * PAIRS)
            for j in steps(pool, CPAIRS):
                for k in range(2):
                    gather_src(LAYERS, j, k, GR_flat, True)
            for j in steps(pool, CPAIRS):
                for k in range(2):
                    gather_dst_and_put(LAYERS, j, k, SR_flat, out, NODES, out_done, 0)

        @block.vector
        def _(dve):
            taken = [0]

            def after(ins):
                ins.then_inc(dve_step, 1)
                taken[0] += 1
                dve.wait_ge(dve_step, taken[0])

            dve.wait_ge(ids_in, 96)
            for slot, row in ((0, 0), (2, 3)):
                after(dve.tensor_copy(id_float[:, row, :], id_rows[:, slot, :]))
            after(dve.tensor_copy(same_next[:, :], id_rows[:, 1, :]))
            after(dve.tensor_tensor(same_next[:, :], same_next[:, :], id_float[:, 0, :], ALU.is_equal))
            after(dve.scalar_tensor_tensor(id_float[:, 1, :], same_next[:, :], float(FAR), id_float[:, 0, :], ALU.mult, ALU.add))
            dve.tensor_scalar(id_float[:, 2, :], id_float[:, 1, :], float(NODES), None, ALU.is_lt).then_inc(ids_done, 1)
            dve.wait_ge(ids_T, 4)
            after(dve.tensor_copy(dst_c[:, :], psZ[:, 0:TILES]))
            after(dve.tensor_scalar(dst_i[:, :], dst_c[:, :], float(NODES - 1), None, ALU.min))
            after(dve.tensor_copy(put_i[:, :], psZ[:, 128:128 + TILES]))
            after(dve.tensor_copy(rep_c[:, :], psZ[:, 256:256 + TILES]))
            after(dve.tensor_copy(src_i[:, :], psZ[:, 384:384 + TILES]))
            dve.wait_ge(bc_in, 16)
            flat = A[:, :, :].rearrange("p t d -> p (t d)").bitcast(I32)
            dve.tensor_scalar(sel_all[:, :], flat[0:TILES, :], id_float[:, 0, P - 1:P], None, ALU.is_equal).then_inc(sel_raw, 1)
            with dve.Fori(0, TILES // 2) as t:
                for u in range(2):
                    dve.tensor_scalar(eq_all[:, ds(t * 2 * P + u * P, P)], flat[:, ds(t * 2 * P + u * P, P)],
                                      dst_c[:, ds(2 * t + u, 1)], None, ALU.is_equal)
            dve.wait_ge(const_in, 48)
            dve.wait_ge(ident_up, 1)
            dve.tensor_tensor(lin[:, 0, :], lin[:, 0, :], ident[:, :], ALU.add)
            dve.wait_ge(wcT_up, 1)
            dve.tensor_copy(wcT[:, :], psG[:, 0:D]).then_inc(tables, 1)

            def add_gram(n):
                dve.wait_ge(gram_up[1], n + 1)
                dve.wait_ge(gram_add, n)
                dve.tensor_tensor(gram[:, :], gram[:, :], psG[:, 0:D + 1], ALU.add).then_inc(gram_add, 1)

            dve.wait_ge(ident_up, 1)

            def add_x_gram(c):
                dve.wait_ge(x_gram, c + 1)
                dve.wait_ge(x_add, c)
                dve.tensor_tensor(gram[:, :], gram[:, :], psG[:, 0:D + 1], ALU.add).then_inc(x_add, 1)

            def make_msg(l, j, k, last=False):
                n = l * CPAIRS + j
                dve.wait_ge(src_in[k], 16 * CT * (n + 1))
                dve.wait_ge(ea_in[k], 16 * (n + 1))
                if last:
                    dve.wait_ge(ea_tail_in, 16 * (l + 1))
                dve.wait_ge(tile_sum[k], n)
                dve.tensor_tensor(msg[k][:, :, :], got[k][:, :, :], ea[k][:, :, :], ALU.add).then_inc(got_used[k], 1)
                dve.wait_ge(got_used[k], l * 2 * CPAIRS + j + 1)
                dve.tensor_scalar(msg[k][:, :, :], msg[k][:, :, :], 0.0, None, ALU.max).then_inc(msg_up[k], 1)

            def make_total(l, j, k, done, base):
                dve.wait_ge(carry_sum[k], l * CPAIRS + j + 1)
                dve.wait_ge(done[k], 16 * CT * (base * CPAIRS + j))
                for b, (lo, hi) in enumerate(HALVES):
                    ins = dve.tensor_tensor(tot[k][:, lo:hi, :], A[:, ds((2 * j + k) * CT + lo, hi - lo), :],
                                            psU[:, 2 * k + b, 0:(hi - lo) * D].rearrange("p (t d) -> p t d", d=D), ALU.add)
                return ins

            def make_mix(l, j, k):
                n = l * CPAIRS + j
                dve.wait_ge(dst_in[k], 16 * CT * (n + 1))
                dve.tensor_scalar(got[k][:, :, :], got[k][:, :, :], self_w[:, 0:1], None, ALU.mult).then_inc(got_scaled[k], 1)
                dve.wait_ge(got_scaled[k], n + 1)
                dve.wait_ge(tot_up[k], n + 1)
                dve.scalar_tensor_tensor(mix[k][:, :, 0:D], tot[k][:, :, :], 0.5, got[k][:, :, :], ALU.mult, ALU.add).then_inc(got_used[k], 1)
                dve.wait_ge(got_used[k], l * 2 * CPAIRS + CPAIRS + j + 1)
                rep = rep_c[:, ds((2 * j + k) * CT, CT)]
                dve.tensor_tensor(mix[k][:, :, 0:D], mix[k][:, :, 0:D], rep.unsqueeze(2).to_broadcast([P, CT, D]), ALU.mult).then_inc(mix_up[k], 1)
                dve.tensor_copy(mix[k][:, :, D:D + 1], rep.unsqueeze(2)).then_inc(mix_up[k], 1)
                dve.wait_ge(cross_sum[k], n + 1)
                dve.wait_ge(cross_add, 2 * n + k)
                dve.tensor_tensor(cross[:, :], cross[:, :], psH[0][:, 0:D + 1], ALU.add).then_inc(cross_add, 1)

            def sum_z(n):
                for k in range(2):
                    dve.wait_ge(rows_in[k], 32 * (n + 1))
                    dve.wait_ge(z_T[k], n)
                    dve.scalar_tensor_tensor(z[k][:, :], hrow[k][:, :], self_w[:, 0:1], arow[k][:, :], ALU.mult, ALU.add).then_inc(z_up[k], 1)

            def bias_pair(n):
                for k in range(2):
                    dve.wait_ge(h_sum[k], n + 1)
                    dve.wait_ge(h_up[k], n)
                    dve.tensor_tensor(hsum[k][:, :, :], psH[k][:, :].rearrange("p (r d) -> p r d", d=D),
                                      b2_bc[:, :, :].to_broadcast([P, R, D]), ALU.add).then_inc(h_bias[k], 1)

            for l in range(LAYERS):
                done = [0]

                def step(ins):
                    ins.then_inc(bn_step, 1)
                    done[0] += 1
                    dve.wait_ge(bn_step, l * BN_STEPS + done[0])

                dve.wait_ge(weights_in, 16 * BATCH_DMAS * (l + 1))
                step(dve.tensor_scalar(self_w[:, 0:1], eps_in[:, :], 1.0, None, ALU.add))
                step(dve.tensor_tensor(self_w[:, 1:2], self_w[:, 0:1], self_w[:, 0:1], ALU.mult))
                for j in steps(dve, CPAIRS - 1):
                    for k in range(2):
                        make_msg(l, j, k)
                        if l == 0:
                            add_x_gram(2 * j + k)
                for k in range(2):
                    make_msg(l, CPAIRS - 1, k, last=k == 1)
                    if l == 0:
                        add_x_gram(2 * (CPAIRS - 1) + k)
                for j in steps(dve, CPAIRS):
                    for k in range(2):
                        make_total(l, j, k, put_done, l).then_inc(tot_up[k], 1)
                        make_mix(l, j, k)
                dve.wait_ge(cross_add, 2 * CPAIRS * (l + 1))
                dve.wait_ge(x_add, 2 * CPAIRS)
                dve.wait_ge(gram_add, PAIRS * l)
                step(dve.scalar_tensor_tensor(zz[:, :], gram[:, 0:D], self_w[:, 1:2], cross[:, 0:D], ALU.mult, ALU.add))
                step(dve.scalar_tensor_tensor(zmean[:, :], gram[:, D:D + 1], self_w[:, 0:1], cross[:, D:D + 1], ALU.mult, ALU.add))
                dve.wait_ge(cross_T, l + 1)
                step(dve.tensor_tensor(zz[:, :], zz[:, :], psZ[:, 0:D], ALU.add))
                step(dve.tensor_scalar(zmean[:, :], zmean[:, :], INV_N, None, ALU.mult))
                step(dve.memset(gram[:, :], 0.0))
                step(dve.memset(cross[:, :], 0.0))
                dve.tensor_scalar(zz[:, :], zz[:, :], INV_N, None, ALU.mult).then_inc(zz_up, 1)
                dve.wait_ge(zzw, l + 1)
                dve.tensor_tensor(zw[:, :], w1[:, :], psZ[:, 0:2 * D], ALU.mult).then_inc(zw_up, 1)
                dve.wait_ge(bn_sums, l + 1)
                step(dve.tensor_copy(bn_mu[:, :], psG[:, 2:4]))
                step(dve.tensor_tensor(bn_sq[:, :], bn_mu[:, :], bn_mu[:, :], ALU.mult))
                step(dve.tensor_tensor(bn_var[:, :], psG[:, 0:2], bn_sq[:, :], ALU.subtract))
                dve.tensor_scalar(bn_var[:, :], bn_var[:, :], 0.0, EPS, ALU.max, ALU.add).then_inc(bn_var_up, 1)
                dve.wait_ge(bn_std_up, l + 1)
                step(dve.reciprocal(bn_scale[:, :], bn_std[:, :]))
                step(dve.tensor_tensor(bn_scale[:, :], bn_scale[:, :], bn_in[:, 1, :], ALU.mult))
                step(dve.tensor_tensor(bn_mu[:, :], bn_mu[:, :], bn_in[:, 0, :], ALU.add))
                step(dve.tensor_tensor(bn_mu[:, :], bn_in[:, 0, :], bn_mu[:, :], ALU.subtract))
                step(dve.tensor_tensor(bn_mu[:, :], bn_mu[:, :], bn_scale[:, :], ALU.mult))
                dve.tensor_tensor(bn_bias[:, :], bn_mu[:, :], bn_in[:, 2, :], ALU.add).then_inc(bn_up, 1)
                assert done[0] == BN_STEPS
                sum_z(l * PAIRS)
                for i in steps(dve, PAIRS - 1):
                    sum_z(l * PAIRS + i + 1)
                    bias_pair(l * PAIRS + i)
                    if l < LAYERS - 1:
                        add_gram(l * PAIRS + i)
                bias_pair(l * PAIRS + PAIRS - 1)
                if l < LAYERS - 1:
                    add_gram(l * PAIRS + PAIRS - 1)

            def layer_norm(i, k, half, src_t):
                stat, var = ((f_stat, f_var), (f_stat2, f_var2))[half]
                for r in range(R):
                    last = dve.bn_stats(fstat[k][:, half, r, :], src_t[:, r, :])
                last.then_inc(stat[k], 1)
                dve.wait_ge(stat[k], i + 1)
                dve.wait_ge((f_x2[k], f_o[k])[half], i)
                plain(dve)
                for r in range(R):
                    last = dve.bn_aggr(fmv[k][:, half, r, :], fstat[k][:, half, r, :])
                last.then_inc(var[k], 1)

            def finish_norm(i, k, half):
                std, rec, norm = ((f_std, f_rec, f_norm), (f_std2, f_rec2, f_norm2))[half]
                dve.wait_ge(std[k], i + 1)
                dve.reciprocal(fstd[k][:, half, :], fstd[k][:, half, :]).then_inc(rec[k], 1)
                dve.wait_ge(rec[k], i + 1)
                dve.scalar_tensor_tensor(fnm[k][:, half, :], fmv[k][:, half, :, 0], -1.0, fstd[k][:, half, :],
                                         ALU.mult, ALU.mult).then_inc(norm[k], 1)

            def front(i, k):
                dve.wait_ge(f_lin[k], i + 1)
                dve.wait_ge(f_x2[k], i)
                dve.tensor_tensor(fy[k][:, :, :], psU[:, k, :].rearrange("p (r d) -> p r d", d=D),
                                  linb_bc[:, :, :].to_broadcast([P, R, D]), ALU.add).then_inc(f_y[k], 1)
                dve.wait_ge(f_y[k], i + 1)
                layer_norm(i, k, 0, fy[k])

            def back(i, k):
                dve.wait_ge(f_w[k], i + 1)
                dve.wait_ge(f_stored[k], 48 * i)
                dve.tensor_tensor(fs[k], psH[k][:, :].rearrange("p (r d) -> p r d", d=D), fx2[k], ALU.add).then_inc(f_s[k], 1)
                dve.wait_ge(f_s[k], i + 1)
                layer_norm(i, k, 1, fs[k])

            group_steps(dve, ((lambda i, k: finish_norm(i, k, 0), -1), (lambda i, k: finish_norm(i, k, 1), -4), (back, -3), (front, 0)))

            for j in steps(dve, CPAIRS):
                for k in range(2):
                    n = 2 * j + k
                    make_total(LAYERS, j, k, out_done, 0).then_inc(e_y, 1)
                    dve.wait_ge(dst_in[k], 16 * CT * (LAYERS * CPAIRS + j + 1))
                    dve.wait_ge(e_y, 2 * n + 1)
                    dve.tensor_tensor(mix[k][:, :, 0:D], tot[k][:, :, :], got[k][:, :, :], ALU.add).then_inc(got_used[k], 1)
                    dve.wait_ge(got_used[k], 2 * CPAIRS * LAYERS + j + 1)
                    for t in range(CT):
                        last = dve.bn_stats(estat[:, t, :], mix[k][:, t, 0:D])
                    last.then_inc(e_stat, 1)
                    dve.wait_ge(e_stat, n + 1)
                    plain(dve)
                    for t in range(CT):
                        last = dve.bn_aggr(emv[:, t, :], estat[:, t, :])
                    last.then_inc(e_var, 1)
                    dve.wait_ge(e_std, n + 1)
                    dve.reciprocal(estd[:, :], estd[:, :]).then_inc(e_rec, 1)
                    dve.wait_ge(e_rec, n + 1)
                    dve.scalar_tensor_tensor(enm[:, :], emv[:, :, 0], -1.0, estd[:, :], ALU.mult, ALU.mult).then_inc(e_nm, 1)
                    dve.wait_ge(e_nm, n + 1)
                    for t in range(CT):
                        last = dve.tensor_scalar(tot[k][:, t, :], mix[k][:, t, 0:D], estd[:, t:t + 1], enm[:, t:t + 1], ALU.mult, ALU.add)
                    last.then_inc(e_y, 1)
                    dve.wait_ge(e_y, 2 * n + 2)
                    dve.sem_inc(tot_up[k], 1)

        @block.tensor
        def _(pe):
            pe.wait_ge(ident_up, 1)
            pe.wait_ge(ids_done, 1)
            for row in range(4):
                pe.transpose(psZ[:, row * P:row * P + TILES], id_float[:, row, :], ident[0:TILES, 0:TILES]).then_inc(ids_T, 1)
            pe.wait_ge(const_in, 48)
            pe.transpose(psG[:, 0:P], wc_in[:, :], ident[:, :]).then_inc(wcT_up, 1)
            pe.wait_ge(tables, 1)

            def gram_pair(n, tail):
                pe.wait_ge(gram_add, n)
                for k in range(2):
                    pe.wait_ge(h_up[k], n + 1)
                    parts = TAIL_P if tail and k == 1 else P
                    for r in range(R):
                        last = pe.matmul(psG[:, 0:D + 1], hp[k][0:parts, r, 0:D], hp[k][0:parts, r, 0:D + 1],
                                         start=k == 0 and r == 0, stop=k == 1 and r == R - 1)
                    last.then_inc(gram_up[k], 1)

            def x_gram_sums(j, k, tail=False):
                c = 2 * j + k
                pe.wait_ge(x_add, c)
                for q in range(XS):
                    pe.wait_ge(x_in[q], 16 * (c + 1))
                    parts = TAIL_P if tail and q == XS - 1 else P
                    for r in range(R):
                        last = pe.matmul(psG[:, 0:D + 1], xg[q][0:parts, r, 0:D], xg[q][0:parts, r, 0:D + 1],
                                         start=q == 0 and r == 0, stop=q == XS - 1 and r == R - 1)
                last.then_inc(x_gram, 1)

            def tile_sums(l, j, k, final=False):
                n = l * CPAIRS + j
                if final:
                    pe.wait_ge(src_in[k], 16 * CT * (n + 1))
                else:
                    pe.wait_ge(msg_up[k], n + 1)
                pe.wait_ge(sel_up[k], l * 2 * CPAIRS + j + 1)
                pe.wait_ge(a_up[k], 2 * n)
                rows = got[k] if final else msg[k]
                for t in range(CT):
                    last = pe.matmul(psU[:, 2 * k + t // 4, (t % 4) * D:(t % 4 + 1) * D], sel[k][:, t * P:(t + 1) * P], rows[:, t, :],
                                     start=True, stop=True)
                last.then_inc(tile_sum[k], 1)

            def carry_sums(l, j, k):
                pe.wait_ge(sel_up[k], l * 2 * CPAIRS + CPAIRS + j + 1)
                for t in range(CT):
                    last = pe.matmul(psU[:, 2 * k + t // 4, (t % 4) * D:(t % 4 + 1) * D], sel[k][0:TILES, t * P:(t + 1) * P],
                                     last_rows[:, :], start=True, stop=True)
                last.then_inc(carry_sum[k], 1)

            def cross_sums(l, j, k):
                n = l * CPAIRS + j
                pe.wait_ge(mix_up[k], 2 * (n + 1))
                pe.wait_ge(cross_add, 2 * n + k)
                for t in range(CT):
                    last = pe.matmul(psH[0][:, 0:D + 1], tot[k][:, t, :], mix[k][:, t, 0:D + 1], start=t == 0, stop=t == CT - 1)
                last.then_inc(cross_sum[k], 1)

            def transposes(n, k):
                pe.wait_ge(z_up[k], n + 1)
                pe.wait_ge(zT_up[1 - k], n + k)
                for r in range(R):
                    last = pe.transpose(psZ[:, r * P:(r + 1) * P], z[k][:, r * D:(r + 1) * D], ident[:, :])
                last.then_inc(z_T[k], 1)

            def up(n, k):
                pe.wait_ge(zT_up[k], n + 1)
                for c in range(2):
                    pe.wait_ge(v_up[k], 2 * n + c if c == 0 else 2 * n)
                    pe.matmul(psU[:, 2 * k + c, :], w1[:, c * D:(c + 1) * D], zT[k][:, :], start=True, stop=True).then_inc(u_up[k], 1)

            def down(n, k):
                pe.wait_ge(v_up[k], 2 * n + 2)
                pe.wait_ge(h_bias[k], n)
                for r in range(R):
                    for c in range(2):
                        last = pe.matmul(psH[k][:, r * D:(r + 1) * D], vT[k][:, c, r * P:(r + 1) * P], w2[:, c, :],
                                         start=c == 0, stop=c == 1)
                last.then_inc(h_sum[k], 1)

            for l in range(LAYERS):
                for j in steps(pe, CPAIRS - 1):
                    for k in range(2):
                        tile_sums(l, j, k)
                        if l == 0:
                            x_gram_sums(j, k)
                for k in range(2):
                    tile_sums(l, CPAIRS - 1, k)
                    if l == 0:
                        x_gram_sums(CPAIRS - 1, k, tail=k == 1)
                pe.wait_ge(last_in, 16 * (l + 1))
                for k in range(2):
                    pe.wait_ge(a_up[k], 2 * CPAIRS * (l + 1))
                for j in steps(pe, CPAIRS):
                    for k in range(2):
                        pe.wait_ge(tot_up[k], l * CPAIRS + j)
                        carry_sums(l, j, k)
                        cross_sums(l, j, k)
                pe.wait_ge(cross_add, 2 * CPAIRS * (l + 1))
                pe.transpose(psZ[:, 0:P], cross[:, 0:D], ident[:, :]).then_inc(cross_T, 1)
                pe.wait_ge(zz_up, l + 1)
                pe.matmul(psZ[:, 0:2 * D], zz[:, :], w1[:, :], start=True, stop=True).then_inc(zzw, 1)
                pe.wait_ge(zw_up, l + 1)
                for c in range(2):
                    pe.matmul(psG[:, c:c + 1], zw[:, c * D:(c + 1) * D], ones[:, :], start=True, stop=True)
                for c in range(2):
                    last = pe.matmul(psG[:, 2 + c:3 + c], w1[:, c * D:(c + 1) * D], zmean[:, :], start=True, stop=True)
                last.then_inc(bn_sums, 1)
                n = l * PAIRS
                transposes(n, 0)
                transposes(n, 1)
                pe.wait_ge(bn_up, l + 1)
                for i in steps(pe, PAIRS - 1):
                    m = l * PAIRS + i
                    up(m, 0)
                    transposes(m + 1, 0)
                    up(m, 1)
                    transposes(m + 1, 1)
                    down(m, 0)
                    down(m, 1)
                    if l < LAYERS - 1:
                        gram_pair(m, False)
                m = l * PAIRS + PAIRS - 1
                up(m, 0)
                up(m, 1)
                down(m, 0)
                down(m, 1)
                if l < LAYERS - 1:
                    gram_pair(m, True)

            def transpose_h(i, k):
                pe.wait_ge(f_in[k], 64 * (i + 1))
                for y in range(LAYERS + 1):
                    bank = (psZ, psG)[y % 2]
                    pe.wait_ge(f_copied[y % 2], 4 * i + 2 * k + y // 2)
                    for r in range(R):
                        last = pe.transpose(bank[:, r * P:(r + 1) * P], fh[k][y][:, r, :], ident[:, :])
                    last.then_inc(f_T[y % 2], 1)

            def linear(i, k):
                for half in range(2):
                    pe.wait_ge(f_copied[half], 4 * i + 2 * k + 2)
                pe.wait_ge(f_y[k], i)
                for r in range(R):
                    for y in range(LAYERS + 1):
                        last = pe.matmul(psU[:, k, r * D:(r + 1) * D], fT[k][:, 4 * y + r, :], lin[:, y, :],
                                         start=y == 0, stop=y == LAYERS)
                last.then_inc(f_lin[k], 1)

            def transpose_x2(i, k):
                pe.wait_ge(f_x2[k], i + 1)
                pe.wait_ge(f_x2c[k], i)
                for r in range(R):
                    last = pe.transpose(psU[:, 2 + k, r * P:(r + 1) * P], fx2[k][:, r, :], ident[:, :])
                last.then_inc(f_x2T[k], 1)

            def convolve(i, k):
                pe.wait_ge(f_x2c[k], i + 1)
                pe.wait_ge(f_s[k], i)
                pe.wait_ge(f_g[k], i)
                for r in range(R):
                    last = pe.matmul(psH[k][:, r * D:(r + 1) * D], fx2T[k][:, r * P:(r + 1) * P], wcT[:, :], start=True, stop=True)
                last.then_inc(f_w[k], 1)

            group_steps(pe, ((transpose_h, 1), (transpose_x2, -2), (linear, 0), (convolve, -2)))

            for j in steps(pe, CPAIRS):
                for k in range(2):
                    tile_sums(LAYERS, j, k, final=True)
            pe.wait_ge(last_in, 16 * (LAYERS + 1))
            for k in range(2):
                pe.wait_ge(a_up[k], 2 * CPAIRS * (LAYERS + 1))
            for j in steps(pe, CPAIRS):
                for k in range(2):
                    pe.wait_ge(tot_up[k], LAYERS * CPAIRS + j)
                    carry_sums(LAYERS, j, k)

        @block.scalar
        def _(act):
            def edge_chunk(l, j, k):
                n = l * CPAIRS + j
                c = (2 * j + k) * CT
                act.wait_ge(tile_sum[k], n)
                act.wait_ge(carry_sum[k], l * CPAIRS)
                act.copy(sel[k][:, :], eq_all[:, ds(c * P, CT * P)]).then_inc(sel_up[k], 1)
                act.wait_ge(tile_sum[k], n + 1)
                for b, (lo, hi) in enumerate(HALVES):
                    act.copy(A[:, ds(c + lo, hi - lo), :], psU[:, 2 * k + b, 0:(hi - lo) * D].rearrange("p (t d) -> p t d", d=D)).then_inc(a_up[k], 1)

            def carry_chunk(l, j, k):
                act.wait_ge(tile_sum[k], (l + 1) * CPAIRS)
                act.wait_ge(carry_sum[k], l * CPAIRS + j)
                act.copy(sel[k][0:TILES, :], sel_all[:, ds((2 * j + k) * CT * P, CT * P)]).then_inc(sel_up[k], 1)

            def copy_z(n, k):
                act.wait_ge(z_T[k], n + 1)
                act.wait_ge(u_up[k], 2 * n)
                act.copy(zT[k][:, :], psZ[:, :]).then_inc(zT_up[k], 1)

            def relu_u(n, k):
                for c in range(2):
                    act.wait_ge(u_up[k], 2 * n + c + 1)
                    act.wait_ge(h_sum[k], n)
                    act.activation(vT[k][:, c, :], psU[:, 2 * k + c, :], ACT.Relu, bias=bn_bias[:, c:c + 1],
                                   scale=bn_scale[:, c:c + 1]).then_inc(v_up[k], 1)

            def relu_h(l, n, k):
                act.wait_ge(h_bias[k], n + 1)
                act.wait_ge(gram_up[k], n if l < LAYERS - 1 else (LAYERS - 1) * PAIRS)
                act.wait_ge(stored[k], 16 * n)
                act.activation(hp[k][:, :, 0:D], hsum[k][:, :, :], ACT.Relu).then_inc(h_up[k], 1)

            act.wait_ge(tables, 1)
            act.wait_ge(sel_done, 1)
            for l in range(LAYERS):
                for j in steps(act, CPAIRS):
                    for k in range(2):
                        edge_chunk(l, j, k)
                for j in steps(act, CPAIRS):
                    for k in range(2):
                        carry_chunk(l, j, k)
                act.wait_ge(bn_var_up, l + 1)
                act.activation(bn_std[:, :], bn_var[:, :], ACT.Sqrt).then_inc(bn_std_up, 1)
                n = l * PAIRS
                copy_z(n, 0)
                copy_z(n, 1)
                act.wait_ge(bn_up, l + 1)
                for i in steps(act, PAIRS - 1):
                    m = l * PAIRS + i
                    for k in range(2):
                        relu_u(m, k)
                        copy_z(m + 1, k)
                    for k in range(2):
                        relu_h(l, m, k)
                for k in range(2):
                    relu_u(l * PAIRS + PAIRS - 1, k)
                for k in range(2):
                    relu_h(l, l * PAIRS + PAIRS - 1, k)

            def root(i, k, half):
                act.wait_ge((f_var, f_var2)[half][k], i + 1)
                act.activation(fstd[k][:, half, :], fmv[k][:, half, :, 1], ACT.Sqrt, bias=eps_c[:, :]).then_inc((f_std, f_std2)[half][k], 1)

            def copy_h(i, k):
                act.wait_ge(f_lin[k], i)
                for y in range(LAYERS + 1):
                    act.wait_ge(f_T[y % 2], 4 * i + 2 * k + y // 2 + 1)
                    act.copy(fT[k][:, 4 * y:4 * y + 4, :], (psZ, psG)[y % 2][:, :].rearrange("p (r d) -> p r d", d=D)).then_inc(f_copied[y % 2], 1)

            def copy_x2(i, k):
                act.wait_ge(f_x2T[k], i + 1)
                act.wait_ge(f_w[k], i)
                act.copy(fx2T[k][:, :], psU[:, 2 + k, :]).then_inc(f_x2c[k], 1)

            def copy_g(i, k):
                act.wait_ge(f_w[k], i + 1)
                act.wait_ge(f_s[k], i + 1)
                act.wait_ge(f_stored[k], 48 * i)
                act.copy(fg[k][:, :], psH[k][:, :]).then_inc(f_g[k], 1)

            group_steps(act, ((copy_h, 1), (lambda i, k: root(i, k, 0), -1), (lambda i, k: root(i, k, 1), -4), (copy_x2, -2),
                              (copy_g, -3)))

            for j in steps(act, CPAIRS):
                for k in range(2):
                    edge_chunk(LAYERS, j, k)
            for j in steps(act, CPAIRS):
                for k in range(2):
                    carry_chunk(LAYERS, j, k)
                    act.wait_ge(e_var, 2 * j + k + 1)
                    act.activation(estd[:, :], emv[:, :, 1], ACT.Sqrt, bias=eps_c[:, :]).then_inc(e_std, 1)


_INS = ["x", "src", "dst", "edge_attr_128", "L0_gnn_eps", "L0_gnn_W1", "L0_gnn_b1", "L0_gnn_gamma", "L0_gnn_beta",
        "L0_gnn_W2", "L0_gnn_b2", "L0_gnn_lin_w", "L0_gnn_lin_b", "L1_gnn_W"]


def kernel(**inputs):
    import numpy as _np
    import concourse.bacc as _bacc
    from concourse import mybir as _mybir
    from concourse.bass_utils import run_bass_kernel_spmd as _run

    nc = _bacc.Bacc("TRN2", target_bir_lowering=False, num_devices=1)
    arrays, args = {}, []
    for name in _INS:
        a = _np.ascontiguousarray(inputs[name])
        arrays[f"in_{name}"] = a
        args.append(nc.dram_tensor(f"in_{name}", a.shape, _mybir.dt.from_np(a.dtype), kind="ExternalInput").ap())
    result = nc.dram_tensor("out_rows", (NODES, D), F32, kind="ExternalOutput").ap()
    gnn_kernel(nc, *args, result)
    r = _run(nc, [arrays], core_ids=[0])
    return r.results[0]["out_rows"]
```

```python
from contextlib import ExitStack

import concourse.bass as bass
from concourse import mybir

F32 = mybir.dt.float32
I32 = mybir.dt.int32
BF16 = mybir.dt.bfloat16
ALU = mybir.AluOpType
ACT = mybir.ActivationFunctionType

P = 128
D = 128
NODES = 50000
EDGES = 12500
LAYERS = 3
R = 4
GROUP = P * R
GROUPS = -(-NODES // GROUP)
PAIRS = GROUPS // 2
ROWS = GROUPS * GROUP
TAIL_P = (NODES - (GROUPS - 1) * GROUP) // R
TILES = -(-EDGES // P)
TAIL_E = EDGES - (TILES - 1) * P
CT = 7
CPAIRS = TILES // CT // 2
FAR = 1 << 20
INV_N = 1.0 / NODES
EPS = 1e-5
HALVES = ((0, 4), (4, 7))
BATCH_DMAS = 6
XS = GROUPS // (2 * CPAIRS)
X_LAG = 4
BN_STEPS = 14


def steps(eng, end, peeled=1):
    yield from range(peeled)
    with eng.Fori(peeled, end) as i:
        yield i


def group_steps(eng, stages):
    def step(i, k):
        for do, lead in stages:
            t = k + lead
            if not isinstance(i, int) or 0 <= 2 * i + t < GROUPS:
                do(i + t // 2, t % 2)

    head, tail = 3, PAIRS - 1
    step(-1, 1)
    for s in range(2 * head):
        step(s // 2, s % 2)
    with eng.Fori(head, tail) as i:
        step(i, 0)
        step(i, 1)
    for s in range(2 * tail, 2 * tail + 6):
        step(s // 2, s % 2)


def gnn_kernel(nc, x, src, dst, edge_attr, eps, W1, b1, gamma, beta, W2, b2, lin_w, lin_b, Wc, out):
    ds = bass.ds
    H = [None] + [nc.dram_tensor(f"h{l}_rows", [GROUPS, P, R * D], F32).ap() for l in range(1, LAYERS + 1)]
    Z = nc.dram_tensor("z_rows", [GROUPS, P, R * D], F32).ap()
    HD = nc.dram_tensor("h_at_dst", [2 * CPAIRS, P, CT * D], F32).ap()
    GR = nc.dram_tensor("g_rows", [GROUPS, P, R * D], F32).ap()
    LAST = nc.dram_tensor("last_rows_dram", [1, TILES, D], F32).ap()
    H_flat = [x] + [h.rearrange("g p (r d) -> (g p r) d", r=R) for h in H[1:]]
    Z_flat = Z.rearrange("g p (r d) -> (g p r) d", r=R)
    GR_flat = GR.rearrange("g p (r d) -> (g p r) d", r=R)
    BODY = (GROUPS - 1) * GROUP
    x_groups = x[0:BODY, :].rearrange("(g p r) d -> g p r d", p=P, r=R)
    x_tail = x[BODY:NODES, :].rearrange("(p r) d -> p r d", r=R)
    out_groups = out[0:BODY, :].rearrange("(g p r) d -> g p (r d)", p=P, r=R)
    out_tail = out[BODY:NODES, :].rearrange("(p r) d -> p (r d)", r=R)
    ea_tiles = edge_attr[0:(TILES - 1) * P, :].rearrange("(t p) d -> p t d", p=P)

    with ExitStack() as ctx:
        def sb(name, shape, dt=F32):
            return ctx.enter_context(nc.sbuf_tensor(name, shape, dt))

        def sem(name):
            return ctx.enter_context(nc.semaphore(name))

        def sems(name, n=2):
            return [sem(f"{name}{k}") for k in range(n)]

        def bufs(name, shape, dt=F32):
            return [sb(f"{name}{k}", shape, dt) for k in range(2)]

        ident = sb("ident", [P, P])
        eq_all = sb("eq_all", [P, TILES * P], BF16)
        sel_all = sb("sel_all", [TILES, TILES * P], BF16)
        later = sb("later", [TILES, TILES], BF16)
        id_rows = sb("id_rows", [TILES, 3, P], I32)
        id_float = sb("id_float", [TILES, 4, P])
        same_next = sb("same_next", [TILES, P])
        dst_c = sb("dst_c", [P, TILES])
        rep_c = sb("rep_c", [P, TILES])
        src_i = sb("src_i", [P, TILES], I32)
        dst_i = sb("dst_i", [P, TILES], I32)
        put_i = sb("put_i", [P, TILES], I32)
        w1 = sb("w1", [P, 2 * D])
        w2 = sb("w2", [P, 2, D])
        lin = sb("lin", [P, LAYERS + 1, D])
        wc_in = sb("wc_in", [P, D])
        wcT = sb("wcT", [P, D])
        b2_bc = sb("b2_bc", [P, 1, D])
        linb_bc = sb("linb_bc", [P, 1, D])
        bn_in = sb("bn_in", [P, 3, 2])
        eps_in = sb("eps_in", [P, LAYERS])
        self_w = sb("self_w", [P, LAYERS])
        pair_end = sb("pair_end", [1, PAIRS], I32)
        pair_end_f = sb("pair_end_f", [1, PAIRS])
        first_dst = sb("first_dst", [1, 2 * CPAIRS])
        put_need_f = sb("put_need_f", [1, 2, PAIRS])
        put_need = sb("put_need", [1, 2, PAIRS], I32)
        reach = sb("reach", [1, 2 * CPAIRS], I32)
        gram = sb("gram", [P, D + 1])
        cross = sb("cross", [P, D + 1])
        zz = sb("zz", [P, D])
        zmean = sb("zmean", [P, 1])
        zw = sb("zw", [P, 2 * D])
        ones = sb("ones", [P, 1])
        eps_c = sb("eps_c", [P, 1])
        bn_mu = sb("bn_mu", [P, 2])
        bn_sq = sb("bn_sq", [P, 2])
        bn_var = sb("bn_var", [P, 2])
        bn_std = sb("bn_std", [P, 2])
        bn_scale = sb("bn_scale", [P, 2])
        bn_bias = sb("bn_bias", [P, 2])
        A = sb("A", [P, TILES, D])
        last_rows = sb("last_rows", [TILES, D])
        got = bufs("got", [P, CT, D])
        ea = bufs("ea", [P, CT, D])
        msg = bufs("msg", [P, CT, D])
        sel = bufs("sel", [P, CT * P])
        tot = bufs("tot", [P, CT, D])
        mix = bufs("mix", [P, CT, D + 2])
        get_ix = bufs("get_ix", [P, CT], I32)
        put_ix = bufs("put_ix", [P, CT], I32)
        estat = bufs("estat", [P, CT, 6])
        emv = bufs("emv", [P, CT, 2])
        estd = bufs("estd", [P, CT])
        enm = bufs("enm", [P, CT])
        z_new = bufs("z_new", [P, R, D + 4])
        z = bufs("z", [P, R * D])
        zT = bufs("zT", [P, R * D])
        vT = bufs("vT", [P, 2, R * D])
        hsum = bufs("hsum", [P, R, D])
        hp = bufs("hp", [P, R, D])
        xg = [t[:, 0:R, :] for t in z_new + mix] + [sb(f"xg{q}", [P, R, D + 2])[:, :, :] for q in range(4, XS)]
        fh = [[A[:, (4 * (4 * k + y)):(4 * (4 * k + y)) + 4, :] for y in range(4)] for k in range(2)]
        fT = [A[:, 32 + 16 * k:48 + 16 * k, :] for k in range(2)]
        fstat = [sb(f"fstat{k}", [P, 2, R, 6]) for k in range(2)]
        fmv = [sb(f"fmv{k}", [P, 2, R, 2]) for k in range(2)]
        fstd = [sb(f"fstd{k}", [P, 2, R]) for k in range(2)]
        fnm = [sb(f"fnm{k}", [P, 2, R]) for k in range(2)]
        fy = hsum
        fx2 = [t[:, 0:R, :] for t in msg]
        fx2T = z
        fg = hp
        fs = [t[:, 0:R * D].rearrange("p (r d) -> p r d", d=D) for t in sel]
        fo = [t[:, 0:R, :] for t in ea]

        psZ = ctx.enter_context(nc.psum_tensor("psZ", [P, 512], F32))
        psU = ctx.enter_context(nc.psum_tensor("psU", [P, 4, 512], F32))
        psH = [ctx.enter_context(nc.psum_tensor(f"psH{k}", [P, 512], F32)) for k in range(2)]
        psG = ctx.enter_context(nc.psum_tensor("psG", [P, 512], F32))

        ids_in = sem("ids_in"); ids_pad = sem("ids_pad"); consts = sem("consts"); passed = sem("passed"); ident_up = sem("ident_up")
        const_in = sem("const_in"); bc_in = sem("bc_in"); w_up = sem("w_up")
        ids_done = sem("ids_done"); ids_T = sem("ids_T"); sel_done = sem("sel_done")
        tables = sem("tables"); setup_done = sem("setup_done"); wcT_up = sem("wcT_up"); dve_step = sem("dve_step"); bc_pad = sem("bc_pad")
        x_in = sems("x_in", XS); x_used = sem("x_used"); x_scaled = sem("x_scaled"); z_built = sems("z_built", XS); x_add = sem("x_add")
        weights_in = sem("weights_in"); staged_src = sem("staged_src"); staged_dst = sem("staged_dst"); staged_put = sem("staged_put")
        dst_ix = sem("dst_ix"); src_ix = sem("src_ix"); hd_stored = sems("hd_stored"); hd_in = sems("hd_in"); hd_scaled = sem("hd_scaled"); pair_end_up = sem("pair_end_up")
        z_rows = sem("z_rows"); put_copied = sem("put_copied"); z_stored = sems("z_stored"); z_new_up = sems("z_new_up"); mixed = sem("mixed")
        src_in = sems("src_in"); ea_in = sems("ea_in"); ea_tail_in = sem("ea_tail_in")
        msg_up = sems("msg_up"); sel_up = sems("sel_up"); tile_sum = sems("tile_sum"); a_up = sems("a_up")
        last_in = sem("last_in"); last_out = sem("last_out"); carry_sum = sems("carry_sum"); dst_in = sems("dst_in")
        tot_up = sems("tot_up"); put_done = sems("put_done"); mix_up = sems("mix_up"); cross_sum = sems("cross_sum")
        cross_add = sem("cross_add"); got_used = sems("got_used")
        cross_T = sem("cross_T"); zz_up = sem("zz_up"); zzw = sem("zzw"); zw_up = sem("zw_up"); bn_sums = sem("bn_sums")
        bn_var_up = sem("bn_var_up"); bn_std_up = sem("bn_std_up"); bn_up = sem("bn_up")
        rows_in = sems("rows_in"); z_T = sems("z_T"); zT_up = sems("zT_up")
        u_up = sems("u_up"); v_up = sems("v_up"); h_sum = sems("h_sum"); h_bias = sems("h_bias"); h_up = sems("h_up")
        gram_up = sems("gram_up"); gram_add = sem("gram_add"); stored = sems("stored")
        f_in = sems("f_in"); f_T = sems("f_T"); f_copied = sems("f_copied"); f_lin = sems("f_lin"); f_y = sems("f_y")
        f_stat = sem("f_stat"); f_rec = sem("f_rec"); f_var = sem("f_var"); f_std = sem("f_std"); f_norm = sem("f_norm"); f_norm2 = sem("f_norm2"); f_std2 = sem("f_std2"); f_rec2 = sem("f_rec2"); f_stat2 = sem("f_stat2"); f_var2 = sem("f_var2"); f_x2 = sems("f_x2")
        f_x2T = sems("f_x2T"); f_x2c = sems("f_x2c"); f_w = sems("f_w"); f_g = sems("f_g"); f_s = sems("f_s"); f_o = sems("f_o")
        f_stored = sems("f_stored"); o_stored = sems("o_stored"); e_out = sem("e_out"); e_stat = sem("e_stat"); e_var = sem("e_var"); e_std = sem("e_std"); out_put = sems("out_put"); bn_step = sem("bn_step")

        def plain(eng):
            eng.sem_inc(passed, 1)

        block = ctx.enter_context(nc.Block())

        @block.sync
        def _(sp):
            sp.wait_ge(ids_pad, 1)
            whole = (TILES - 1) * P
            for slot, ids in ((0, dst), (2, src)):
                sp.dma_start(id_rows[0:TILES - 1, slot, :], ids[0:whole].rearrange("(t p) -> t p", p=P)).then_inc(ids_in, 16)
                sp.dma_start(id_rows[TILES - 1:TILES, slot, 0:TAIL_E], ids[whole:EDGES].rearrange("(t p) -> t p", t=1)).then_inc(ids_in, 16)
            sp.dma_start(id_rows[0:TILES - 1, 1, :], dst[1:whole + 1].rearrange("(t p) -> t p", p=P)).then_inc(ids_in, 16)
            sp.dma_start(id_rows[TILES - 1:TILES, 1, 0:TAIL_E - 1], dst[whole + 1:EDGES].rearrange("(t p) -> t p", t=1)).then_inc(ids_in, 16)
            sp.wait_ge(bc_pad, 1)
            flat = A[:, :, :].rearrange("p t d -> p (t d)").bitcast(I32)
            sp.dma_start(flat[:, 0:EDGES], dst.partition_broadcast(P)).then_inc(bc_in, 16)
            sp.dma_start(lin[:, :, :], lin_w.rearrange("(y k) d -> k y d", k=D)).then_inc(const_in, 16)
            sp.dma_start(wc_in[:, :], Wc).then_inc(const_in, 16)
            sp.dma_start(linb_bc[:, 0, :], lin_b.partition_broadcast(P)).then_inc(const_in, 16)
            sp.wait_ge(ident_up, 1)

            def store_x(c, q):
                sp.wait_ge(x_scaled, c * XS + q + 1)
                sp.dma_start(Z[ds(c * XS + q, 1), :, :].rearrange("o p (r d) -> (o p) r d", r=R), xg[q][:, :, 0:D]).then_inc(z_built[q], 16)

            def pass_x(c, first=False, tail=False):
                for q in range(XS):
                    if q >= X_LAG:
                        store_x(c, q - X_LAG)
                    elif not first:
                        store_x(c - 1, q - X_LAG + XS)
                    if not first:
                        sp.wait_ge(x_used, (c - 1) * XS + q + 1)
                        plain(sp)
                    sp.wait_ge(z_built[q], 16 * c)
                    plain(sp)
                    if tail and q == XS - 1:
                        sp.dma_start(xg[q][0:TAIL_P, :, 0:D], x_tail).then_inc(x_in[q], 16)
                    else:
                        sp.dma_start(xg[q][:, :, 0:D], x_groups[ds(c * XS + q, 1), :, :, :].rearrange("o p r d -> (o p) r d")).then_inc(x_in[q], 16)

            def load_hd(l, j, k):
                sp.wait_ge(hd_stored[k], 16 * (l * CPAIRS + j + 1))
                plain(sp)
                sp.wait_ge(mix_up[k], 2 * (l * CPAIRS + j))
                sp.wait_ge(msg_up[k], min(l + 1, LAYERS) * CPAIRS)
                sp.dma_start(ea[k][:, :, :], HD[ds(2 * j + k, 1), :, :].rearrange("o p (t d) -> (o p) t d", d=D)).then_inc(hd_in[k], 16)

            def load_ea(l, j, k, last=False):
                sp.wait_ge(msg_up[k], l * CPAIRS + j)
                sp.wait_ge(mix_up[k], 2 * l * CPAIRS)
                c = (2 * j + k) * CT
                if last:
                    sp.dma_start(ea[k][:, 0:CT - 1, :], ea_tiles[:, c:c + CT - 1, :]).then_inc(ea_in[k], 16)
                    sp.dma_start(ea[k][0:TAIL_E, CT - 1, :], edge_attr[(TILES - 1) * P:EDGES, :]).then_inc(ea_tail_in, 16)
                else:
                    sp.dma_start(ea[k][:, :, :], ea_tiles[:, ds(c, CT), :]).then_inc(ea_in[k], 16)

            def load_last_rows(l):
                for k in range(2):
                    sp.wait_ge(a_up[k], 2 * CPAIRS * (l + 1))
                sp.dma_start(LAST, A[P - 1:P, :, :]).then_inc(last_out, 16)
                sp.wait_ge(last_out, 16 * (l + 1))
                sp.dma_start(last_rows[:, :], LAST.rearrange("o t d -> (o t) d")).then_inc(last_in, 16)

            def h_group(y, g, to, done, tail=False):
                if y:
                    sp.dma_start(to, H[y][ds(g, 1), :, :].rearrange("o p (r d) -> (o p) r d", r=R)).then_inc(done, 16)
                elif tail:
                    sp.dma_start(to[0:TAIL_P], x_tail).then_inc(done, 16)
                else:
                    sp.dma_start(to, x_groups[ds(g, 1), :, :, :].rearrange("o p r d -> (o p) r d")).then_inc(done, 16)

            def load_rows(l, n, i):
                for k in range(2):
                    need = sp.value_load(put_need[0:1, k, ds(i, 1)], min_val=16 * CT, max_val=16 * CT * CPAIRS)
                    sp.wait_ge(put_done[k], need + 16 * CT * CPAIRS * l)
                    plain(sp)
                for k in range(2):
                    sp.wait_ge(z_T[k], n)
                    plain(sp)
                    sp.dma_start(z[k][:, :], Z[ds(2 * i + k, 1), :, :].rearrange("o p n -> (o p) n")).then_inc(rows_in[k], 16)

            def store_pair(l, i):
                n = l * PAIRS + i
                for k in range(2):
                    sp.wait_ge(h_up[k], n + 1)
                    sp.dma_start(H[l + 1][ds(2 * i + k, 1), :, :].rearrange("o p (r d) -> (o p) r d", r=R),
                                 hp[k][:, :, :]).then_inc(stored[k], 16)
                    if l < LAYERS - 1:
                        sp.wait_ge(z_new_up[k], n + 1)
                        sp.dma_start(Z[ds(2 * i + k, 1), :, :].rearrange("o p (r d) -> (o p) r d", r=R),
                                     z_new[k][:, :, 0:D]).then_inc(z_stored[k], 16)

            sp.dma_start(eps_in[:, :], eps.partition_broadcast(P)).then_inc(w_up, 16)
            for c in steps(sp, CPAIRS + 1):
                pass_x(c, first=isinstance(c, int))
            for l in range(LAYERS):
                for k in range(2):
                    if l:
                        sp.wait_ge(stored[k], 16 * PAIRS * l)
                        sp.wait_ge(z_stored[k], 16 * PAIRS * l)
                sp.dma_start(w1[:, :], W1[l]).then_inc(weights_in, 16)
                sp.dma_start(w2[:, :, :], W2[l].rearrange("(c k) n -> k c n", c=2)).then_inc(weights_in, 16)
                for row, vec in enumerate((b1, gamma, beta)):
                    with nc.allow_non_contiguous_dma("256 features"):
                        sp.dma_start(bn_in[:, row, :], vec[l].rearrange("(c f) -> f c", c=2)).then_inc(weights_in, 16)
                sp.dma_start(b2_bc[:, 0, :], b2[l].partition_broadcast(P)).then_inc(weights_in, 16)
                for j in steps(sp, CPAIRS - 1):
                    load_ea(l, j, 0)
                    if l == 0 and not isinstance(j, int):
                        pass_x(CPAIRS + j)
                    load_ea(l, j, 1)
                load_ea(l, CPAIRS - 1, 0)
                if l == 0:
                    c = 2 * CPAIRS - 1
                    pass_x(c, tail=True)
                    for q in range(XS - X_LAG, XS):
                        store_x(c, q)
                load_ea(l, CPAIRS - 1, 1, last=True)
                load_last_rows(l)
                for j in steps(sp, CPAIRS):
                    for k in range(2):
                        load_hd(l, j, k)
                if l == 0:
                    for q in range(XS):
                        sp.wait_ge(z_built[q], 16 * 2 * CPAIRS)
                load_rows(l, l * PAIRS, 0)
                load_rows(l, l * PAIRS + 1, 1)
                for i in steps(sp, PAIRS - 3):
                    load_rows(l, l * PAIRS + i + 2, i + 2)
                    store_pair(l, i)
                load_rows(l, (l + 1) * PAIRS - 1, PAIRS - 1)
                store_pair(l, PAIRS - 3)
                store_pair(l, PAIRS - 2)
                store_pair(l, PAIRS - 1)

            sp.wait_ge(put_copied, 2 * CPAIRS * LAYERS)
            for k in range(2):
                sp.wait_ge(stored[k], 16 * PAIRS * LAYERS)

            def load_f(i, k, last=False):
                if not isinstance(i, int) or i:
                    for half in range(2):
                        sp.wait_ge(f_T[half], 4 * i + 2 * k - 2)
                for y in range(LAYERS + 1):
                    h_group(y, 2 * i + k, fh[k][y], f_in[k], last)

            def store_gs(i, k):
                sp.wait_ge(f_g[k], i + 1)
                sp.dma_start(GR[ds(2 * i + k, 1), :, :].rearrange("o p (r d) -> (o p) r d", r=R), fg[k][:, :, :]).then_inc(f_stored[k], 16)
                sp.wait_ge(f_s[k], i + 1)
                sp.dma_start(Z[ds(2 * i + k, 1), :, :].rearrange("o p (r d) -> (o p) r d", r=R), fs[k]).then_inc(f_stored[k], 16)

            def store_out(i, k, tail=False):
                sp.wait_ge(f_o[k], i + 1)
                if tail:
                    sp.dma_start(out_tail.rearrange("p (r d) -> p r d", r=R), fo[k][0:TAIL_P]).then_inc(o_stored[k], 16)
                else:
                    sp.dma_start(out_groups[ds(2 * i + k, 1), :, :].rearrange("o p (r d) -> (o p) r d", r=R), fo[k]).then_inc(o_stored[k], 16)

            ahead = 7
            for g in range(ahead):
                load_f(g // 2, g % 2)
            for i in steps(sp, (GROUPS - 1 - ahead) // 2):
                for k in range(2):
                    store_gs(i, k)
                    load_f(i + (k + ahead) // 2, (k + ahead) % 2)
                    store_out(i, k)
            for g in range((GROUPS - 1 - ahead) // 2 * 2, GROUPS):
                store_gs(g // 2, g % 2)
                if g + ahead < GROUPS:
                    load_f((g + ahead) // 2, (g + ahead) % 2, last=g + ahead == GROUPS - 1)
                store_out(g // 2, g % 2, tail=g == GROUPS - 1)
            load_last_rows(LAYERS)
            for k in range(2):
                sp.wait_ge(f_stored[k], 32 * PAIRS)
                sp.wait_ge(o_stored[k], 16 * PAIRS)
            for j in steps(sp, CPAIRS):
                for k in range(2):
                    load_hd(LAYERS, j, k)
            for k in range(2):
                sp.wait_ge(out_put[k], 16 * CT * CPAIRS)

        @block.gpsimd
        def _(pool):
            taken = [0]

            def after(ins):
                taken[0] += 1
                ins.then_inc(consts, 1)
                pool.wait_ge(consts, taken[0])

            after(pool.memset(id_rows[:, 0, :], FAR))
            after(pool.memset(id_rows[:, 1, :], -1))
            pool.memset(id_rows[:, 2, :], 0).then_inc(ids_pad, 1)
            flat = A[:, :, :].rearrange("p t d -> p (t d)").bitcast(I32)
            pool.memset(flat[:, EDGES:TILES * P], FAR).then_inc(bc_pad, 1)
            pool.iota(pair_end[:, :], pattern=[[2 * GROUP, PAIRS]], base=2 * GROUP, channel_multiplier=0).then_inc(pair_end_up, 1)
            after(pool.memset(ident[:, :], 0.0))
            after(pool.affine_select(out=ident[:, :], in_=ident[:, :], compare_op=ALU.not_equal, fill=1.0, base=0,
                                     pattern=[[-1, P]], channel_multiplier=1))
            after(pool.memset(ones[:, :], 1.0))
            after(pool.memset(eps_c[:, :], EPS))
            for k in range(2):
                after(pool.memset(z_new[k][:, :, :], 1.0))
                after(pool.memset(mix[k][:, :, :], 1.0))
                after(pool.memset(ea[k][:, :, :], 0.0))
            for q in range(4, XS):
                after(pool.memset(xg[q], 1.0))
            after(pool.memset(gram[:, :], 0.0))
            after(pool.memset(later[:, :], 1.0))
            after(pool.affine_select(out=later[:, :], in_=later[:, :], compare_op=ALU.is_gt, fill=0.0, base=0,
                                     pattern=[[1, TILES]], channel_multiplier=-1))
            pool.memset(cross[:, :], 0.0).then_inc(ident_up, 1)
            def stage(table, ix, c, done, n):
                pool.tensor_copy(ix[:, :], table[:, ds(c * CT, CT)]).then_inc(done, 1)
                pool.wait_ge(done, n)
                plain(pool)

            def gather(rows, to, ix, done):
                for t in range(CT):
                    pool.indirect_dma_start(to[:, t, :], None, rows, bass.IndirectOffsetOnAxis(ix[:, t:t + 1], 0),
                                            bounds_check=rows.shape[0] - 1, oob_is_err=False).then_inc(done, 16)

            def scatter(rows, ix, target, done):
                for t in range(CT):
                    pool.indirect_dma_start(target, bass.IndirectOffsetOnAxis(ix[:, t:t + 1], 0), rows[:, t, :], None,
                                            bounds_check=NODES - 1, oob_is_err=False).then_inc(done, 16)

            def gather_src(l, j, k, rows):
                if l < LAYERS:
                    pool.wait_ge(hd_stored[k], 16 * (CPAIRS * (l + 1) - 1))
                    pool.wait_ge(got_used[k], l * CPAIRS + j)
                else:
                    pool.wait_ge(hd_stored[k], 16 * (CPAIRS * (l + 1) - 1))
                    pool.wait_ge(tile_sum[k], l * CPAIRS + j)
                c = 2 * j + k
                stage(src_i, get_ix[k], c, staged_src, l * 2 * CPAIRS + c + 1)
                gather(rows, got[k], get_ix[k], src_in[k])

            def gather_dst(l, j, k, rows, last=False):
                c = 2 * j + k
                if l:
                    need = pool.value_load(reach[0:1, ds(c, 1)], min_val=16, max_val=16 * PAIRS)
                    for kk in range(2):
                        if l < LAYERS:
                            pool.wait_ge(z_stored[kk], need + 16 * PAIRS * (l - 1))
                        else:
                            pool.wait_ge(f_stored[kk], need * 2)
                if last and l == LAYERS:
                    pool.wait_ge(tile_sum[k], (l + 1) * CPAIRS)
                elif l or last:
                    pool.wait_ge(got_used[k], (l + last) * CPAIRS)
                pool.wait_ge(hd_stored[k], 16 * (l * CPAIRS + j))
                plain(pool)
                stage(dst_i, get_ix[k], c, staged_dst, l * 2 * CPAIRS + c + 1)
                gather(rows, got[k], get_ix[k], dst_in[k])

            def store_hd(l, j, k):
                pool.wait_ge(dst_in[k], 16 * CT * (l * CPAIRS + j + 1))
                plain(pool)
                pool.dma_start(HD[ds(2 * j + k, 1), :, :].rearrange("o p (t d) -> (o p) t d", d=D), got[k][:, :, :]).then_inc(hd_stored[k], 16)

            def gather_all_dst(l, rows):
                gather_dst(l, 0, 0, rows)
                gather_dst(l, 0, 1, rows)
                store_hd(l, 0, 0)
                with pool.Fori(1, CPAIRS - 1) as j:
                    gather_dst(l, j, 0, rows)
                    store_hd(l, j - 1, 1)
                    gather_dst(l, j, 1, rows)
                    store_hd(l, j, 0)
                store_hd(l, CPAIRS - 2, 1)

            def gather_all_src(l, rows, rows_dst):
                for j in steps(pool, CPAIRS):
                    for k in range(2):
                        gather_src(l, j, k, rows)
                for k in range(2):
                    gather_dst(l, CPAIRS - 1, k, rows_dst, last=True)
                for k in range(2):
                    store_hd(l, CPAIRS - 1, k)

            def put_rows(l, j, k):
                c = 2 * j + k
                n = l * 2 * CPAIRS + c + 1
                pool.wait_ge(put_done[k], 16 * CT * (l * CPAIRS + j))
                pool.wait_ge(z_rows, n)
                plain(pool)
                pool.tensor_copy(msg[k][:, :, :], A[:, ds(c * CT, CT), :]).then_inc(put_copied, 1)
                stage(put_i, put_ix[k], c, staged_put, n)
                pool.wait_ge(put_copied, n)
                plain(pool)
                scatter(msg[k], put_ix[k], Z_flat, put_done[k])

            pool.wait_ge(dst_ix, 1)
            gather_all_dst(0, x)
            pool.wait_ge(src_ix, 1)
            for l in range(LAYERS):
                for k in range(2):
                    if l:
                        pool.wait_ge(stored[k], 16 * PAIRS * l)
                        pool.wait_ge(z_stored[k], 16 * PAIRS * l)
                gather_all_src(l, H_flat[l], Z_flat if l else x)
                if l == 0:
                    for q in range(XS):
                        pool.wait_ge(z_built[q], 16 * 2 * CPAIRS)
                for j in steps(pool, CPAIRS):
                    for k in range(2):
                        put_rows(l, j, k)
                gather_all_dst(l + 1, Z_flat)

            for k in range(2):
                pool.wait_ge(f_stored[k], 32 * PAIRS)
                pool.wait_ge(o_stored[k], 16 * PAIRS)
            gather_all_src(LAYERS, GR_flat, Z_flat)
            for j in steps(pool, CPAIRS):
                for k in range(2):
                    c = 2 * j + k
                    pool.wait_ge(out_put[k], 16 * CT * j)
                    plain(pool)
                    stage(put_i, put_ix[k], c, staged_put, LAYERS * 2 * CPAIRS + c + 1)
                    pool.wait_ge(e_out, c + 1)
                    plain(pool)
                    scatter(msg[k], put_ix[k], out, out_put[k])

        @block.vector
        def _(dve):
            taken = [0]

            def after(ins):
                ins.then_inc(dve_step, 1)
                taken[0] += 1
                dve.wait_ge(dve_step, taken[0])

            dve.wait_ge(ids_in, 96)
            for slot, row in ((0, 0), (2, 3)):
                after(dve.tensor_copy(id_float[:, row, :], id_rows[:, slot, :]))
            after(dve.tensor_copy(same_next[:, :], id_rows[:, 1, :]))
            after(dve.tensor_tensor(same_next[:, :], same_next[:, :], id_float[:, 0, :], ALU.is_equal))
            after(dve.scalar_tensor_tensor(id_float[:, 1, :], same_next[:, :], float(FAR), id_float[:, 0, :], ALU.mult, ALU.add))
            dve.tensor_scalar(id_float[:, 2, :], id_float[:, 1, :], float(NODES), None, ALU.is_lt).then_inc(ids_done, 1)
            dve.wait_ge(ids_T, 4)
            after(dve.tensor_copy(dst_c[:, :], psZ[:, 0:TILES]))
            dve.tensor_scalar(dst_i[:, :], dst_c[:, :], float(NODES - 1), None, ALU.min).then_inc(dst_ix, 1)
            after(dve.tensor_copy(put_i[:, :], psZ[:, 128:128 + TILES]))
            after(dve.tensor_copy(rep_c[:, :], psZ[:, 256:256 + TILES]))
            dve.tensor_copy(src_i[:, :], psZ[:, 384:384 + TILES]).then_inc(src_ix, 1)
            dve.wait_ge(bc_in, 16)
            flat = A[:, :, :].rearrange("p t d -> p (t d)").bitcast(I32)
            dve.tensor_scalar(sel_all[:, :], flat[0:TILES, :], id_float[:, 0, P - 1:P], None, ALU.is_equal)
            dve.wait_ge(const_in, 48)
            dve.wait_ge(ident_up, 1)
            dve.tensor_tensor(lin[:, 0, :], lin[:, 0, :], ident[:, :], ALU.add)
            dve.wait_ge(wcT_up, 1)
            dve.tensor_copy(wcT[:, :], psG[:, 0:D]).then_inc(setup_done, 1)

            def add_gram(n):
                dve.wait_ge(gram_up[1], n + 1)
                dve.wait_ge(gram_add, n)
                dve.tensor_tensor(gram[:, :], gram[:, :], psG[:, 0:D + 1], ALU.add).then_inc(gram_add, 1)

            dve.wait_ge(ident_up, 1)

            def scale_x(c):
                for q in range(XS):
                    dve.wait_ge(x_in[q], 16 * (c + 1))
                    dve.tensor_scalar(xg[q][:, :, 0:D], xg[q][:, :, 0:D], self_w[:, 0:1], None, ALU.mult).then_inc(x_scaled, 1)
                dve.wait_ge(x_used, (c + 1) * XS)
                dve.wait_ge(x_add, c)
                dve.tensor_tensor(gram[:, :], gram[:, :], psG[:, 0:D + 1], ALU.add).then_inc(x_add, 1)

            def make_msg(l, j, k, last=False):
                n = l * CPAIRS + j
                dve.wait_ge(src_in[k], 16 * CT * (n + 1))
                dve.wait_ge(ea_in[k], 16 * (n + 1))
                if last:
                    dve.wait_ge(ea_tail_in, 16 * (l + 1))
                dve.wait_ge(tile_sum[k], n)
                dve.tensor_tensor(msg[k][:, :, :], got[k][:, :, :], ea[k][:, :, :], ALU.add).then_inc(got_used[k], 1)
                dve.wait_ge(got_used[k], l * CPAIRS + j + 1)
                dve.tensor_scalar(msg[k][:, :, :], msg[k][:, :, :], 0.0, None, ALU.max).then_inc(msg_up[k], 1)

            def make_total(l, j, k):
                dve.wait_ge(carry_sum[k], l * CPAIRS + j + 1)
                for b, (lo, hi) in enumerate(HALVES):
                    ins = dve.tensor_tensor(tot[k][:, lo:hi, :], A[:, ds((2 * j + k) * CT + lo, hi - lo), :],
                                            psU[:, 2 * k + b, 0:(hi - lo) * D].rearrange("p (t d) -> p t d", d=D), ALU.add)
                return ins

            def make_mix(l, j, k):
                n = l * CPAIRS + j
                c = 2 * j + k
                dve.wait_ge(hd_in[k], 16 * (n + 1))
                if l == 0:
                    dve.tensor_scalar(ea[k][:, :, :], ea[k][:, :, :], self_w[:, 0:1], None, ALU.mult).then_inc(hd_scaled, 1)
                    dve.wait_ge(hd_scaled, c + 1)
                dve.wait_ge(tot_up[k], n + 1)
                dve.scalar_tensor_tensor(mix[k][:, :, 0:D], tot[k][:, :, :], 0.5, ea[k][:, :, :], ALU.mult, ALU.add).then_inc(mixed, 1)
                dve.tensor_tensor(A[:, ds(c * CT, CT), :], tot[k][:, :, :], ea[k][:, :, :], ALU.add).then_inc(z_rows, 1)
                dve.wait_ge(z_rows, l * 2 * CPAIRS + c + 1)
                dve.wait_ge(mixed, l * 2 * CPAIRS + c + 1)
                rep = rep_c[:, ds(c * CT, CT)]
                dve.tensor_tensor(mix[k][:, :, 0:D], mix[k][:, :, 0:D], rep.unsqueeze(2).to_broadcast([P, CT, D]), ALU.mult).then_inc(mix_up[k], 1)
                dve.tensor_copy(mix[k][:, :, D:D + 1], rep.unsqueeze(2)).then_inc(mix_up[k], 1)

            def add_cross(l, j, k):
                n = l * CPAIRS + j
                dve.wait_ge(cross_sum[k], n + 1)
                dve.wait_ge(cross_add, 2 * n + k)
                dve.tensor_tensor(cross[:, :], cross[:, :], psH[k][:, 0:D + 1], ALU.add).then_inc(cross_add, 1)

            def finish_pair(l, n):
                for k in range(2):
                    dve.wait_ge(h_sum[k], n + 1)
                    dve.wait_ge(h_up[k], n)
                    dve.tensor_tensor(hsum[k][:, :, :], psH[k][:, :].rearrange("p (r d) -> p r d", d=D),
                                      b2_bc[:, :, :].to_broadcast([P, R, D]), ALU.add).then_inc(h_bias[k], 1)
                    if l < LAYERS - 1:
                        dve.wait_ge(h_bias[k], n + 1)
                        dve.wait_ge(gram_up[k], n)
                        dve.wait_ge(z_stored[k], 16 * n)
                        dve.tensor_scalar(z_new[k][:, :, 0:D], hsum[k][:, :, :], 0.0, self_w[:, l + 1:l + 2], ALU.max, ALU.mult).then_inc(z_new_up[k], 1)

            dve.wait_ge(w_up, 16)
            after(dve.tensor_scalar(self_w[:, :], eps_in[:, :], 1.0, None, ALU.add))
            def mask_sel(c):
                part = sel_all[:, ds(c * 2 * CT * P, 2 * CT * P)].rearrange("j (t e) -> j t e", e=P)
                mask = later[:, ds(c * 2 * CT, 2 * CT)]
                dve.tensor_tensor(part, part, mask.unsqueeze(2).to_broadcast([TILES, 2 * CT, P]), ALU.mult).then_inc(sel_done, 1)

            def compare(c):
                for u in range(2 * CT):
                    t = c * 2 * CT + u
                    dve.tensor_scalar(eq_all[:, ds(t * P, P)], flat[:, ds(t * P, P)], dst_c[:, ds(t, 1)], None, ALU.is_equal)

            for c in steps(dve, CPAIRS):
                compare(c)
                mask_sel(c)
                scale_x(c)
            scale_x(CPAIRS)
            chunks = flat[0:1, :].rearrange("o (c e) -> o c e", e=CT * P)
            after(dve.tensor_copy(first_dst[:, :], chunks[:, :, 0]))
            after(dve.tensor_scalar(reach[:, :], chunks[:, :, CT * P - 1], float(NODES - 1), None, ALU.min))
            after(dve.tensor_scalar(reach[:, :], reach[:, :], (2 * GROUP).bit_length() - 1, None, ALU.arith_shift_right))
            after(dve.tensor_scalar(reach[:, :], reach[:, :], 16.0, 16.0, ALU.mult, ALU.add))
            dve.wait_ge(pair_end_up, 1)
            after(dve.tensor_copy(pair_end_f[:, :], pair_end[:, :]))
            after(dve.memset(put_need_f[:, :, :], 0.0))
            for c in range(2 * CPAIRS):
                after(dve.scalar_tensor_tensor(put_need_f[:, c % 2, :], pair_end_f[:, :], first_dst[:, c:c + 1], put_need_f[:, c % 2, :],
                                               ALU.is_gt, ALU.add))
            dve.tensor_scalar(put_need[:, :, :], put_need_f[:, :, :], 1.0, float(16 * CT), ALU.max, ALU.mult).then_inc(tables, 1)
            for l in range(LAYERS):
                done = [0]

                def step(ins):
                    ins.then_inc(bn_step, 1)
                    done[0] += 1
                    dve.wait_ge(bn_step, l * BN_STEPS + done[0])

                dve.wait_ge(weights_in, 16 * BATCH_DMAS * (l + 1))
                for j in steps(dve, CPAIRS - 1):
                    make_msg(l, j, 0)
                    if l == 0 and not isinstance(j, int):
                        scale_x(CPAIRS + j)
                    make_msg(l, j, 1)
                make_msg(l, CPAIRS - 1, 0)
                if l == 0:
                    scale_x(2 * CPAIRS - 1)
                make_msg(l, CPAIRS - 1, 1, last=True)
                for j in steps(dve, CPAIRS):
                    for k in range(2):
                        make_total(l, j, k).then_inc(tot_up[k], 1)
                        make_mix(l, j, k)
                    for k in range(2):
                        add_cross(l, j, k)
                dve.wait_ge(cross_add, 2 * CPAIRS * (l + 1))
                dve.wait_ge(x_add, 2 * CPAIRS)
                dve.wait_ge(gram_add, PAIRS * l)
                step(dve.tensor_tensor(zz[:, :], gram[:, 0:D], cross[:, 0:D], ALU.add))
                step(dve.tensor_tensor(zmean[:, :], gram[:, D:D + 1], cross[:, D:D + 1], ALU.add))
                dve.wait_ge(cross_T, l + 1)
                step(dve.tensor_tensor(zz[:, :], zz[:, :], psZ[:, 0:D], ALU.add))
                step(dve.tensor_scalar(zmean[:, :], zmean[:, :], INV_N, None, ALU.mult))
                step(dve.memset(gram[:, :], 0.0))
                step(dve.memset(cross[:, :], 0.0))
                dve.tensor_scalar(zz[:, :], zz[:, :], INV_N, None, ALU.mult).then_inc(zz_up, 1)
                dve.wait_ge(zzw, l + 1)
                dve.tensor_tensor(zw[:, :], w1[:, :], psZ[:, 0:2 * D], ALU.mult).then_inc(zw_up, 1)
                dve.wait_ge(bn_sums, l + 1)
                step(dve.tensor_copy(bn_mu[:, :], psG[:, 2:4]))
                step(dve.tensor_tensor(bn_sq[:, :], bn_mu[:, :], bn_mu[:, :], ALU.mult))
                step(dve.tensor_tensor(bn_var[:, :], psG[:, 0:2], bn_sq[:, :], ALU.subtract))
                dve.tensor_scalar(bn_var[:, :], bn_var[:, :], 0.0, EPS, ALU.max, ALU.add).then_inc(bn_var_up, 1)
                dve.wait_ge(bn_std_up, l + 1)
                step(dve.reciprocal(bn_scale[:, :], bn_std[:, :]))
                step(dve.tensor_tensor(bn_scale[:, :], bn_scale[:, :], bn_in[:, 1, :], ALU.mult))
                step(dve.tensor_tensor(bn_mu[:, :], bn_mu[:, :], bn_in[:, 0, :], ALU.add))
                step(dve.tensor_tensor(bn_mu[:, :], bn_in[:, 0, :], bn_mu[:, :], ALU.subtract))
                step(dve.tensor_tensor(bn_mu[:, :], bn_mu[:, :], bn_scale[:, :], ALU.mult))
                dve.tensor_tensor(bn_bias[:, :], bn_mu[:, :], bn_in[:, 2, :], ALU.add).then_inc(bn_up, 1)
                assert done[0] == BN_STEPS
                for i in steps(dve, PAIRS, peeled=2):
                    if l < LAYERS - 1 and not (isinstance(i, int) and i == 0):
                        add_gram(l * PAIRS + i - 1)
                    finish_pair(l, l * PAIRS + i)
                if l < LAYERS - 1:
                    add_gram(l * PAIRS + PAIRS - 1)

            def rows_stat(i, k, half):
                dve.wait_ge((f_y[k], f_s[k])[half], i + 1)
                for r in range(R):
                    last = dve.bn_stats(fstat[k][:, half, r, :], (fy, fs)[half][k][:, r, :])
                last.then_inc((f_stat, f_stat2)[half], 1)

            def rows_aggregate(i, k, half):
                dve.wait_ge((f_stat, f_stat2)[half], 2 * i + k + 1)
                dve.wait_ge((f_x2[k], f_o[k])[half], i)
                plain(dve)
                for r in range(R):
                    last = dve.bn_aggr(fmv[k][:, half, r, :], fstat[k][:, half, r, :])
                last.then_inc((f_var, f_var2)[half], 1)

            def rows_rstd(i, k, half):
                dve.wait_ge((f_std, f_std2)[half], 2 * i + k + 1)
                dve.reciprocal(fstd[k][:, half, :], fstd[k][:, half, :]).then_inc((f_rec, f_rec2)[half], 1)

            def rows_shift(i, k, half):
                dve.wait_ge((f_rec, f_rec2)[half], 2 * i + k + 1)
                dve.scalar_tensor_tensor(fnm[k][:, half, :], fmv[k][:, half, :, 0], -1.0, fstd[k][:, half, :],
                                         ALU.mult, ALU.mult).then_inc((f_norm, f_norm2)[half], 1)

            def normalize(i, k, half):
                dve.wait_ge((f_norm, f_norm2)[half], 2 * i + k + 1)
                src_t, dst_t, up = ((fy[k], fx2[k], f_x2[k]), (fs[k], fo[k], f_o[k]))[half]
                if half == 0:
                    dve.wait_ge(f_s[k], i)
                    dve.wait_ge(f_x2T[k], i)
                else:
                    dve.wait_ge(o_stored[k], 16 * i)
                for r in range(R):
                    last = dve.tensor_scalar(dst_t[:, r, :], src_t[:, r, :], fstd[k][:, half, r:r + 1], fnm[k][:, half, r:r + 1],
                                             ALU.mult, ALU.add)
                last.then_inc(up, 1)

            def add_bias(i, k):
                dve.wait_ge(f_lin[k], i + 1)
                dve.wait_ge(f_x2[k], i)
                dve.tensor_tensor(fy[k][:, :, :], psU[:, k, :].rearrange("p (r d) -> p r d", d=D),
                                  linb_bc[:, :, :].to_broadcast([P, R, D]), ALU.add).then_inc(f_y[k], 1)

            def add_conv(i, k):
                dve.wait_ge(f_w[k], i + 1)
                dve.wait_ge(f_stored[k], 32 * i)
                dve.wait_ge(f_o[k], i)
                dve.tensor_tensor(fs[k], psH[k][:, :].rearrange("p (r d) -> p r d", d=D), fx2[k], ALU.add).then_inc(f_s[k], 1)

            def of(do, half):
                return lambda i, k: do(i, k, half)

            group_steps(dve, ((of(rows_rstd, 0), -1), (add_conv, -3), (of(rows_shift, 0), -1), (of(rows_rstd, 1), -4),
                              (of(rows_stat, 1), -3), (of(normalize, 0), -1), (of(rows_shift, 1), -4), (of(rows_aggregate, 1), -3),
                              (add_bias, 0), (of(normalize, 1), -4), (of(rows_stat, 0), 0), (of(rows_aggregate, 0), 0)))

            def edge_stats(j, k):
                n = 2 * j + k
                if not (isinstance(j, int) and j == 0):
                    dve.wait_ge(e_out, n - 1)
                dve.wait_ge(carry_sum[k], LAYERS * CPAIRS + j + 1)
                for b, (lo, hi) in enumerate(HALVES):
                    last = dve.tensor_tensor(mix[k][:, lo:hi, 0:D], A[:, ds(n * CT + lo, hi - lo), :],
                                             psU[:, 2 * k + b, 0:(hi - lo) * D].rearrange("p (t d) -> p t d", d=D), ALU.add)
                last.then_inc(tot_up[k], 1)
                dve.wait_ge(tot_up[k], LAYERS * CPAIRS + j + 1)
                dve.wait_ge(hd_in[k], 16 * (LAYERS * CPAIRS + j + 1))
                dve.tensor_tensor(mix[k][:, :, 0:D], mix[k][:, :, 0:D], ea[k][:, :, :], ALU.add).then_inc(mix_up[k], 2)
                dve.wait_ge(mix_up[k], 2 * (LAYERS * CPAIRS + j + 1))
                for t in range(CT):
                    last = dve.bn_stats(estat[k][:, t, :], mix[k][:, t, 0:D])
                last.then_inc(e_stat, 1)
                dve.wait_ge(e_stat, n + 1)
                plain(dve)
                for t in range(CT):
                    last = dve.bn_aggr(emv[k][:, t, :], estat[k][:, t, :])
                last.then_inc(e_var, 1)

            def edge_norm(j, k):
                n = 2 * j + k
                dve.wait_ge(e_std, n + 1)
                dve.reciprocal(estd[k][:, :], estd[k][:, :]).then_inc(f_rec, 1)
                dve.wait_ge(f_rec, GROUPS + n + 1)
                dve.scalar_tensor_tensor(enm[k][:, :], emv[k][:, :, 0], -1.0, estd[k][:, :], ALU.mult, ALU.mult).then_inc(f_norm, 1)
                dve.wait_ge(f_norm, GROUPS + n + 1)
                dve.wait_ge(out_put[k], 16 * CT * j)
                for t in range(CT):
                    last = dve.tensor_scalar(msg[k][:, t, :], mix[k][:, t, 0:D], estd[k][:, t:t + 1], enm[k][:, t:t + 1], ALU.mult, ALU.add)
                last.then_inc(e_out, 1)

            edge_stats(0, 0)
            for j in steps(dve, CPAIRS - 1):
                edge_stats(j, 1)
                edge_norm(j, 0)
                edge_stats(j + 1, 0)
                edge_norm(j, 1)
            edge_stats(CPAIRS - 1, 1)
            edge_norm(CPAIRS - 1, 0)
            edge_norm(CPAIRS - 1, 1)

        @block.tensor
        def _(pe):
            pe.wait_ge(ident_up, 1)
            pe.wait_ge(ids_done, 1)
            for row in range(4):
                pe.transpose(psZ[:, row * P:row * P + TILES], id_float[:, row, :], ident[0:TILES, 0:TILES]).then_inc(ids_T, 1)
            pe.wait_ge(const_in, 48)
            pe.transpose(psG[:, 0:P], wc_in[:, :], ident[:, :]).then_inc(wcT_up, 1)
            pe.wait_ge(setup_done, 1)

            def gram_pair(n, tail):
                pe.wait_ge(gram_add, n)
                for k in range(2):
                    pe.wait_ge(z_new_up[k], n + 1)
                    parts = TAIL_P if tail and k == 1 else P
                    for r in range(R):
                        last = pe.matmul(psG[:, 0:D + 1], z_new[k][0:parts, r, 0:D], z_new[k][0:parts, r, 0:D + 1],
                                         start=k == 0 and r == 0, stop=k == 1 and r == R - 1)
                    last.then_inc(gram_up[k], 1)

            def x_gram_sums(c, tail=False):
                pe.wait_ge(x_add, c)
                for q in range(XS):
                    pe.wait_ge(x_scaled, c * XS + q + 1)
                    parts = TAIL_P if tail and q == XS - 1 else P
                    for r in range(R):
                        last = pe.matmul(psG[:, 0:D + 1], xg[q][0:parts, r, 0:D], xg[q][0:parts, r, 0:D + 1],
                                         start=q == 0 and r == 0, stop=q == XS - 1 and r == R - 1)
                    last.then_inc(x_used, 1)

            def tile_sums(l, j, k, final=False):
                n = l * CPAIRS + j
                if final:
                    pe.wait_ge(src_in[k], 16 * CT * (n + 1))
                else:
                    pe.wait_ge(msg_up[k], n + 1)
                pe.wait_ge(sel_up[k], l * 2 * CPAIRS + j + 1)
                pe.wait_ge(a_up[k], 2 * n)
                rows = got[k] if final else msg[k]
                for t in range(CT):
                    last = pe.matmul(psU[:, 2 * k + t // 4, (t % 4) * D:(t % 4 + 1) * D], sel[k][:, t * P:(t + 1) * P], rows[:, t, :],
                                     start=True, stop=True)
                last.then_inc(tile_sum[k], 1)

            def carry_sums(l, j, k):
                pe.wait_ge(sel_up[k], l * 2 * CPAIRS + CPAIRS + j + 1)
                for t in range(CT):
                    last = pe.matmul(psU[:, 2 * k + t // 4, (t % 4) * D:(t % 4 + 1) * D], sel[k][0:TILES, t * P:(t + 1) * P],
                                     last_rows[:, :], start=True, stop=True)
                last.then_inc(carry_sum[k], 1)

            def cross_sums(l, j, k):
                n = l * CPAIRS + j
                pe.wait_ge(mix_up[k], 2 * (n + 1))
                pe.wait_ge(cross_add, 2 * n)
                for t in range(CT):
                    last = pe.matmul(psH[k][:, 0:D + 1], tot[k][:, t, :], mix[k][:, t, 0:D + 1], start=t == 0, stop=t == CT - 1)
                last.then_inc(cross_sum[k], 1)

            def transposes(n, k):
                pe.wait_ge(rows_in[k], 16 * (n + 1))
                pe.wait_ge(zT_up[1 - k], n + k)
                for r in range(R):
                    last = pe.transpose(psZ[:, r * P:(r + 1) * P], z[k][:, r * D:(r + 1) * D], ident[:, :])
                last.then_inc(z_T[k], 1)

            def up(n, k):
                pe.wait_ge(zT_up[k], n + 1)
                for c in range(2):
                    pe.wait_ge(v_up[k], 2 * n + c if c == 0 else 2 * n)
                    pe.matmul(psU[:, 2 * k + c, :], w1[:, c * D:(c + 1) * D], zT[k][:, :], start=True, stop=True).then_inc(u_up[k], 1)

            def down(n, k):
                pe.wait_ge(v_up[k], 2 * n + 2)
                pe.wait_ge(h_bias[k], n)
                for r in range(R):
                    for c in range(2):
                        last = pe.matmul(psH[k][:, r * D:(r + 1) * D], vT[k][:, c, r * P:(r + 1) * P], w2[:, c, :],
                                         start=c == 0, stop=c == 1)
                last.then_inc(h_sum[k], 1)

            for c in steps(pe, CPAIRS + 1):
                x_gram_sums(c)
            for l in range(LAYERS):
                for j in steps(pe, CPAIRS - 1):
                    tile_sums(l, j, 0)
                    if l == 0 and not isinstance(j, int):
                        x_gram_sums(CPAIRS + j)
                    tile_sums(l, j, 1)
                tile_sums(l, CPAIRS - 1, 0)
                if l == 0:
                    x_gram_sums(2 * CPAIRS - 1, tail=True)
                tile_sums(l, CPAIRS - 1, 1)
                pe.wait_ge(last_in, 16 * (l + 1))
                for k in range(2):
                    pe.wait_ge(a_up[k], 2 * CPAIRS * (l + 1))
                for k in range(2):
                    carry_sums(l, 0, k)
                for j in steps(pe, CPAIRS - 1):
                    for k in range(2):
                        pe.wait_ge(tot_up[k], l * CPAIRS + j + 1)
                        carry_sums(l, j + 1, k)
                        cross_sums(l, j, k)
                for k in range(2):
                    cross_sums(l, CPAIRS - 1, k)
                pe.wait_ge(cross_add, 2 * CPAIRS * (l + 1))
                pe.transpose(psZ[:, 0:P], cross[:, 0:D], ident[:, :]).then_inc(cross_T, 1)
                pe.wait_ge(zz_up, l + 1)
                pe.matmul(psZ[:, 0:2 * D], zz[:, :], w1[:, :], start=True, stop=True).then_inc(zzw, 1)
                pe.wait_ge(zw_up, l + 1)
                for c in range(2):
                    pe.matmul(psG[:, c:c + 1], zw[:, c * D:(c + 1) * D], ones[:, :], start=True, stop=True)
                for c in range(2):
                    last = pe.matmul(psG[:, 2 + c:3 + c], w1[:, c * D:(c + 1) * D], zmean[:, :], start=True, stop=True)
                last.then_inc(bn_sums, 1)
                n = l * PAIRS
                transposes(n, 0)
                transposes(n, 1)
                pe.wait_ge(bn_up, l + 1)
                for i in steps(pe, PAIRS - 1, peeled=2):
                    m = l * PAIRS + i
                    up(m, 0)
                    transposes(m + 1, 0)
                    if l < LAYERS - 1 and not (isinstance(i, int) and i == 0):
                        gram_pair(m - 1, False)
                    up(m, 1)
                    transposes(m + 1, 1)
                    down(m, 0)
                    down(m, 1)
                m = l * PAIRS + PAIRS - 1
                up(m, 0)
                if l < LAYERS - 1:
                    gram_pair(m - 1, False)
                up(m, 1)
                down(m, 0)
                down(m, 1)
                if l < LAYERS - 1:
                    gram_pair(m, True)

            def transpose_h(i, k, ys):
                pe.wait_ge(f_in[k], 64 * (i + 1))
                for y in ys:
                    bank = (psZ, psG)[y % 2]
                    pe.wait_ge(f_copied[y % 2], 4 * i + 2 * k + y // 2)
                    for r in range(R):
                        last = pe.transpose(bank[:, r * P:(r + 1) * P], fh[k][y][:, r, :], ident[:, :])
                    last.then_inc(f_T[y % 2], 1)

            def linear(i, k):
                for half in range(2):
                    pe.wait_ge(f_copied[half], 4 * i + 2 * k + 2)
                pe.wait_ge(f_y[k], i)
                for r in range(R):
                    for y in range(LAYERS + 1):
                        last = pe.matmul(psU[:, k, r * D:(r + 1) * D], fT[k][:, 4 * y + r, :], lin[:, y, :],
                                         start=y == 0, stop=y == LAYERS)
                last.then_inc(f_lin[k], 1)

            def transpose_x2(i, k):
                pe.wait_ge(f_x2[k], i + 1)
                pe.wait_ge(f_x2c[k], i)
                for r in range(R):
                    last = pe.transpose(psU[:, 2 + k, r * P:(r + 1) * P], fx2[k][:, r, :], ident[:, :])
                last.then_inc(f_x2T[k], 1)

            def convolve(i, k):
                pe.wait_ge(f_x2c[k], i + 1)
                pe.wait_ge(f_s[k], i)
                pe.wait_ge(f_g[k], i)
                for r in range(R):
                    last = pe.matmul(psH[k][:, r * D:(r + 1) * D], fx2T[k][:, r * P:(r + 1) * P], wcT[:, :], start=True, stop=True)
                last.then_inc(f_w[k], 1)

            group_steps(pe, ((lambda i, k: transpose_h(i, k, (0, 1)), 1), (convolve, -3), (lambda i, k: transpose_h(i, k, (2, 3)), 1),
                             (transpose_x2, -2), (linear, 0)))

            for j in steps(pe, CPAIRS):
                for k in range(2):
                    tile_sums(LAYERS, j, k, final=True)
            pe.wait_ge(last_in, 16 * (LAYERS + 1))
            for k in range(2):
                pe.wait_ge(a_up[k], 2 * CPAIRS * (LAYERS + 1))
            for j in steps(pe, CPAIRS):
                for k in range(2):
                    pe.wait_ge(tot_up[k], LAYERS * CPAIRS + j)
                    carry_sums(LAYERS, j, k)

        @block.scalar
        def _(act):
            def edge_chunk(l, j, k):
                n = l * CPAIRS + j
                c = (2 * j + k) * CT
                act.wait_ge(tile_sum[k], n)
                act.wait_ge(carry_sum[k], l * CPAIRS)
                act.copy(sel[k][:, :], eq_all[:, ds(c * P, CT * P)]).then_inc(sel_up[k], 1)
                act.wait_ge(tile_sum[k], n + 1)
                for b, (lo, hi) in enumerate(HALVES):
                    act.copy(A[:, ds(c + lo, hi - lo), :], psU[:, 2 * k + b, 0:(hi - lo) * D].rearrange("p (t d) -> p t d", d=D)).then_inc(a_up[k], 1)

            def carry_chunk(l, j, k):
                act.wait_ge(sel_done, CPAIRS)
                act.wait_ge(tile_sum[k], (l + 1) * CPAIRS)
                act.wait_ge(carry_sum[k], l * CPAIRS + j)
                act.copy(sel[k][0:TILES, :], sel_all[:, ds((2 * j + k) * CT * P, CT * P)]).then_inc(sel_up[k], 1)

            def copy_z(n, k):
                act.wait_ge(z_T[k], n + 1)
                act.wait_ge(u_up[k], 2 * n)
                act.copy(zT[k][:, :], psZ[:, :]).then_inc(zT_up[k], 1)

            def relu_u(n, k):
                for c in range(2):
                    act.wait_ge(u_up[k], 2 * n + c + 1)
                    act.wait_ge(h_sum[k], n)
                    act.activation(vT[k][:, c, :], psU[:, 2 * k + c, :], ACT.Relu, bias=bn_bias[:, c:c + 1],
                                   scale=bn_scale[:, c:c + 1]).then_inc(v_up[k], 1)

            def relu_h(l, n, k):
                act.wait_ge(h_bias[k], n + 1)
                act.wait_ge(stored[k], 16 * n)
                act.activation(hp[k][:, :, :], hsum[k][:, :, :], ACT.Relu).then_inc(h_up[k], 1)

            act.wait_ge(tables, 1)
            for l in range(LAYERS):
                if l:
                    act.wait_ge(put_copied, 2 * CPAIRS * l)
                for j in steps(act, CPAIRS):
                    for k in range(2):
                        edge_chunk(l, j, k)
                for j in steps(act, CPAIRS):
                    for k in range(2):
                        carry_chunk(l, j, k)
                act.wait_ge(bn_var_up, l + 1)
                act.activation(bn_std[:, :], bn_var[:, :], ACT.Sqrt).then_inc(bn_std_up, 1)
                n = l * PAIRS
                copy_z(n, 0)
                copy_z(n, 1)
                act.wait_ge(bn_up, l + 1)
                for i in steps(act, PAIRS - 1):
                    m = l * PAIRS + i
                    for k in range(2):
                        relu_u(m, k)
                        copy_z(m + 1, k)
                    for k in range(2):
                        relu_h(l, m, k)
                for k in range(2):
                    relu_u(l * PAIRS + PAIRS - 1, k)
                for k in range(2):
                    relu_h(l, l * PAIRS + PAIRS - 1, k)

            def root(i, k, half):
                act.wait_ge((f_var, f_var2)[half], 2 * i + k + 1)
                act.activation(fstd[k][:, half, :], fmv[k][:, half, :, 1], ACT.Sqrt, bias=eps_c[:, :]).then_inc((f_std, f_std2)[half], 1)

            def copy_h(i, k):
                act.wait_ge(f_lin[k], i)
                for y in range(LAYERS + 1):
                    act.wait_ge(f_T[y % 2], 4 * i + 2 * k + y // 2 + 1)
                    act.copy(fT[k][:, 4 * y:4 * y + 4, :], (psZ, psG)[y % 2][:, :].rearrange("p (r d) -> p r d", d=D)).then_inc(f_copied[y % 2], 1)

            def copy_x2(i, k):
                act.wait_ge(f_x2T[k], i + 1)
                act.wait_ge(f_w[k], i)
                act.copy(fx2T[k][:, :], psU[:, 2 + k, :]).then_inc(f_x2c[k], 1)

            def copy_g(i, k):
                act.wait_ge(f_w[k], i + 1)
                act.wait_ge(f_s[k], i + 1)
                act.wait_ge(f_stored[k], 32 * i)
                act.copy(fg[k][:, :, :], psH[k][:, :].rearrange("p (r d) -> p r d", d=D)).then_inc(f_g[k], 1)

            group_steps(act, ((copy_h, 1), (lambda i, k: root(i, k, 0), -1), (lambda i, k: root(i, k, 1), -4), (copy_x2, -2),
                              (copy_g, -3)))

            for k in range(2):
                act.wait_ge(f_stored[k], 32 * PAIRS)
                act.wait_ge(f_o[k], PAIRS)
            for j in steps(act, CPAIRS):
                for k in range(2):
                    edge_chunk(LAYERS, j, k)
            for j in steps(act, CPAIRS):
                for k in range(2):
                    carry_chunk(LAYERS, j, k)
                    act.wait_ge(e_var, 2 * j + k + 1)
                    act.activation(estd[k][:, :], emv[k][:, :, 1], ACT.Sqrt, bias=eps_c[:, :]).then_inc(e_std, 1)


_INS = ["x", "src", "dst", "edge_attr_128", "L0_gnn_eps", "L0_gnn_W1", "L0_gnn_b1", "L0_gnn_gamma", "L0_gnn_beta",
        "L0_gnn_W2", "L0_gnn_b2", "L0_gnn_lin_w", "L0_gnn_lin_b", "L1_gnn_W"]


def kernel(**inputs):
    import numpy as _np
    import concourse.bacc as _bacc
    from concourse import mybir as _mybir
    from concourse.bass_utils import run_bass_kernel_spmd as _run

    nc = _bacc.Bacc("TRN2", target_bir_lowering=False, num_devices=1)
    arrays, args = {}, []
    for name in _INS:
        a = _np.ascontiguousarray(inputs[name])
        arrays[f"in_{name}"] = a
        args.append(nc.dram_tensor(f"in_{name}", a.shape, _mybir.dt.from_np(a.dtype), kind="ExternalInput").ap())
    result = nc.dram_tensor("out_rows", (NODES, D), F32, kind="ExternalOutput").ap()
    gnn_kernel(nc, *args, result)
    r = _run(nc, [arrays], core_ids=[0])
    return r.results[0]["out_rows"]
```
